# Optimizing a Trainium2 kernel written in Bass

```python
import numpy as np
import jax
import jax.numpy as jnp

def _softmax(x, axis=-1):
    return jax.nn.softmax(x, axis=axis)

def _gelu(x):
    return jax.nn.gelu(x, approximate=True)

def _silu(x):
    return jax.nn.silu(x)

def _sigmoid(x):
    return jax.nn.sigmoid(x)

def _layernorm(x, axis=-1, eps=1e-05):
    m = jnp.mean(x, axis=axis, keepdims=True)
    v = jnp.var(x, axis=axis, keepdims=True)
    return (x - m) / jnp.sqrt(v + eps)

def _scatter_add(tgt, idx, src, axis=0):
    return tgt.at[idx].add(src)

def _segment_sum(src, seg, n):
    return jax.ops.segment_sum(src, seg, n)
kernel_name = 'mk_seq_postln_d1_jaxref_r4_fb3145'

def setup_inputs(seed: int=0):
    np.random.seed(seed)
    _w = jnp.asarray

    def _L0_attn_setup():
        import jax, jax.numpy as jnp
        import numpy as np
        D_MODEL = 256
        D_STATE = 16
        D_CONV = 4
        EXPAND = 2
        D_INNER = EXPAND * D_MODEL
        DT_RANK = D_MODEL // 16
        BATCH, SEQLEN = (2, 256)

        def _mamba_fwd(hidden_states, in_proj_w, conv1d_w, conv1d_b, x_proj_w, dt_proj_w, dt_proj_b, A_log, D_param, out_proj_w):
            Bsz, L, _ = hidden_states.shape
            xz = jnp.einsum('bld,ed->ble', hidden_states, in_proj_w)
            x, z = jnp.split(xz, 2, axis=-1)
            xc = jnp.transpose(x, (0, 2, 1))
            kern = conv1d_w[:, None, :]
            conv = jax.lax.conv_general_dilated(xc, kern, window_strides=(1,), padding=[(D_CONV - 1, 0)], dimension_numbers=('NCH', 'OIH', 'NCH'), feature_group_count=D_INNER)
            u = jax.nn.silu(conv + conv1d_b[None, :, None])
            ut = jnp.transpose(u, (0, 2, 1))
            x_dbl = jnp.einsum('bld,rd->blr', ut, x_proj_w)
            dt_low = x_dbl[..., :DT_RANK]
            B_var = x_dbl[..., DT_RANK:DT_RANK + D_STATE]
            C_var = x_dbl[..., DT_RANK + D_STATE:]
            delta = jax.nn.softplus(jnp.einsum('blr,dr->bld', dt_low, dt_proj_w) + dt_proj_b)
            A = -jnp.exp(A_log)
            dA = jnp.exp(delta[..., None] * A)
            dBu = delta[..., None] * B_var[:, :, None, :] * ut[..., None]

            def step(h, inp):
                da, dbu, c = inp
                h = da * h + dbu
                y = jnp.einsum('bdn,bn->bd', h, c)
                return (h, y)
            h0 = jnp.zeros((Bsz, D_INNER, D_STATE), dtype=hidden_states.dtype)
            _, ys = jax.lax.scan(step, h0, (jnp.moveaxis(dA, 1, 0), jnp.moveaxis(dBu, 1, 0), jnp.moveaxis(C_var, 1, 0)))
            y = jnp.moveaxis(ys, 0, 1)
            y = y + ut * D_param
            out_z = y * jax.nn.silu(z)
            return jnp.einsum('bld,ed->ble', out_z, out_proj_w)
        key = jax.random.key(seed)
        ks = jax.random.split(key, 9)
        f32 = jnp.float32
        hidden_states = jax.random.normal(ks[0], (BATCH, SEQLEN, D_MODEL), dtype=f32)
        in_proj_w = jax.random.normal(ks[1], (2 * D_INNER, D_MODEL), dtype=f32) * D_MODEL ** (-0.5)
        conv1d_w = jax.random.normal(ks[2], (D_INNER, D_CONV), dtype=f32) * D_CONV ** (-0.5)
        conv1d_b = jax.random.normal(ks[3], (D_INNER,), dtype=f32) * 0.1
        x_proj_w = jax.random.normal(ks[4], (DT_RANK + 2 * D_STATE, D_INNER), dtype=f32) * D_INNER ** (-0.5)
        dt_std = DT_RANK ** (-0.5)
        dt_proj_w = jax.random.uniform(ks[5], (D_INNER, DT_RANK), dtype=f32, minval=-dt_std, maxval=dt_std)
        dt_proj_b = jax.random.normal(ks[6], (D_INNER,), dtype=f32) * 0.1
        A_log = jnp.log(jnp.tile(jnp.arange(1, D_STATE + 1, dtype=f32), (D_INNER, 1)))
        D_param = jnp.ones((D_INNER,), dtype=f32)
        out_proj_w = jax.random.normal(ks[7], (D_MODEL, D_INNER), dtype=f32) * D_INNER ** (-0.5)
        return dict(hidden_states=hidden_states, in_proj_w=in_proj_w, conv1d_w=conv1d_w, conv1d_b=conv1d_b, x_proj_w=x_proj_w, dt_proj_w=dt_proj_w, dt_proj_b=dt_proj_b, A_log=A_log, D_param=D_param, out_proj_w=out_proj_w)
    _L0_attn_in = _L0_attn_setup()

    def _L0_ffn_setup():
        import jax, jax.numpy as jnp
        import numpy as np
        B, S, D = (4, 1024, 256)
        DD = 4 * D
        N_EXPERTS = 8
        CAPACITY = 1.0
        LN_EPS = 1e-05
        key = jax.random.key(seed)
        ks = jax.random.split(key, 8)
        s1 = 1.0 / np.sqrt(D)
        s2 = 1.0 / np.sqrt(DD)
        return {'x': jax.random.normal(ks[0], (B, S, D), jnp.float32), 'gate_w': jax.random.normal(ks[1], (N_EXPERTS, D), jnp.float32) * 0.02, 'ln_w': jnp.ones((D,), jnp.float32), 'ln_b': jnp.zeros((D,), jnp.float32), 'fc1s': jax.random.normal(ks[2], (N_EXPERTS, DD, D), jnp.float32) * s1, 'b1s': jax.random.normal(ks[3], (N_EXPERTS, DD), jnp.float32) * s1, 'fc2s': jax.random.normal(ks[4], (N_EXPERTS, D, DD), jnp.float32) * s2, 'b2s': jax.random.normal(ks[5], (N_EXPERTS, D), jnp.float32) * s2}
    _L0_ffn_in = _L0_ffn_setup()
    _d = {'L0_attn_hidden_states': _L0_attn_in['hidden_states'], 'L0_attn_in_proj_w': _L0_attn_in['in_proj_w'], 'L0_attn_conv1d_w': _L0_attn_in['conv1d_w'], 'L0_attn_conv1d_b': _L0_attn_in['conv1d_b'], 'L0_attn_x_proj_w': _L0_attn_in['x_proj_w'], 'L0_attn_dt_proj_w': _L0_attn_in['dt_proj_w'], 'L0_attn_dt_proj_b': _L0_attn_in['dt_proj_b'], 'L0_attn_A_log': _L0_attn_in['A_log'], 'L0_attn_D_param': _L0_attn_in['D_param'], 'L0_attn_out_proj_w': _L0_attn_in['out_proj_w'], 'L0_ffn_gate_w': _L0_ffn_in['gate_w'], 'L0_ffn_ln_w': _L0_ffn_in['ln_w'], 'L0_ffn_ln_b': _L0_ffn_in['ln_b'], 'L0_ffn_fc1s': _L0_ffn_in['fc1s'], 'L0_ffn_b1s': _L0_ffn_in['b1s'], 'L0_ffn_fc2s': _L0_ffn_in['fc2s'], 'L0_ffn_b2s': _L0_ffn_in['b2s']}
    _x0 = _d['L0_attn_hidden_states']
    _d['L0_attn_hidden_states'] = jax.random.normal(jax.random.fold_in(jax.random.key(seed), 1), (8, 2048, 256), dtype=_x0.dtype)
    del _x0
    return _d

def reference(L0_attn_hidden_states, L0_attn_in_proj_w, L0_attn_conv1d_w, L0_attn_conv1d_b, L0_attn_x_proj_w, L0_attn_dt_proj_w, L0_attn_dt_proj_b, L0_attn_A_log, L0_attn_D_param, L0_attn_out_proj_w, L0_ffn_gate_w, L0_ffn_ln_w, L0_ffn_ln_b, L0_ffn_fc1s, L0_ffn_b1s, L0_ffn_fc2s, L0_ffn_b2s):

    def _L0_attn_ref(hidden_states, in_proj_w, conv1d_w, conv1d_b, x_proj_w, dt_proj_w, dt_proj_b, A_log, D_param, out_proj_w):
        import jax, jax.numpy as jnp
        import numpy as np
        D_MODEL = 256
        D_STATE = 16
        D_CONV = 4
        EXPAND = 2
        D_INNER = EXPAND * D_MODEL
        DT_RANK = D_MODEL // 16
        BATCH, SEQLEN = (2, 256)

        def _mamba_fwd(hidden_states, in_proj_w, conv1d_w, conv1d_b, x_proj_w, dt_proj_w, dt_proj_b, A_log, D_param, out_proj_w):
            Bsz, L, _ = hidden_states.shape
            xz = jnp.einsum('bld,ed->ble', hidden_states, in_proj_w)
            x, z = jnp.split(xz, 2, axis=-1)
            xc = jnp.transpose(x, (0, 2, 1))
            kern = conv1d_w[:, None, :]
            conv = jax.lax.conv_general_dilated(xc, kern, window_strides=(1,), padding=[(D_CONV - 1, 0)], dimension_numbers=('NCH', 'OIH', 'NCH'), feature_group_count=D_INNER)
            u = jax.nn.silu(conv + conv1d_b[None, :, None])
            ut = jnp.transpose(u, (0, 2, 1))
            x_dbl = jnp.einsum('bld,rd->blr', ut, x_proj_w)
            dt_low = x_dbl[..., :DT_RANK]
            B_var = x_dbl[..., DT_RANK:DT_RANK + D_STATE]
            C_var = x_dbl[..., DT_RANK + D_STATE:]
            delta = jax.nn.softplus(jnp.einsum('blr,dr->bld', dt_low, dt_proj_w) + dt_proj_b)
            A = -jnp.exp(A_log)
            dA = jnp.exp(delta[..., None] * A)
            dBu = delta[..., None] * B_var[:, :, None, :] * ut[..., None]

            def step(h, inp):
                da, dbu, c = inp
                h = da * h + dbu
                y = jnp.einsum('bdn,bn->bd', h, c)
                return (h, y)
            h0 = jnp.zeros((Bsz, D_INNER, D_STATE), dtype=hidden_states.dtype)
            _, ys = jax.lax.scan(step, h0, (jnp.moveaxis(dA, 1, 0), jnp.moveaxis(dBu, 1, 0), jnp.moveaxis(C_var, 1, 0)))
            y = jnp.moveaxis(ys, 0, 1)
            y = y + ut * D_param
            out_z = y * jax.nn.silu(z)
            return jnp.einsum('bld,ed->ble', out_z, out_proj_w)
        return _mamba_fwd(hidden_states, in_proj_w, conv1d_w, conv1d_b, x_proj_w, dt_proj_w, dt_proj_b, A_log, D_param, out_proj_w)

    def _L0_ffn_ref(x, gate_w, ln_w, ln_b, fc1s, b1s, fc2s, b2s):
        import jax, jax.numpy as jnp
        import numpy as np
        B, S, D = (4, 1024, 256)
        DD = 4 * D
        N_EXPERTS = 8
        CAPACITY = 1.0
        LN_EPS = 1e-05
        og_shape = x.shape
        d = og_shape[-1]
        xf = x.reshape(-1, d)
        bs = xf.shape[0]
        n = gate_w.shape[0]
        k = int(bs * CAPACITY) // n
        scores = jax.nn.softmax(xf @ gate_w.T, axis=-1)
        vals, idx = jax.lax.top_k(scores.T, k)
        kept_w = vals.T
        kept_idx = idx.T
        flat_idx = kept_idx.reshape(-1)
        y = xf[flat_idx].reshape(k, n, d)
        mu = y.mean(-1, keepdims=True)
        var = ((y - mu) ** 2).mean(-1, keepdims=True)
        y = (y - mu) * jax.lax.rsqrt(var + LN_EPS) * ln_w + ln_b
        h = jnp.einsum('knd,nfd->knf', y, fc1s) + b1s
        h = jax.nn.gelu(h, approximate=True)
        out = jnp.einsum('knf,ndf->knd', h, fc2s) + b2s
        out = out * kept_w[..., None]
        xf = xf.at[flat_idx].add(out.reshape(k * n, d))
        return xf.reshape(og_shape)
    x = L0_attn_hidden_states
    x = _layernorm(x + _L0_attn_ref(x, L0_attn_in_proj_w, L0_attn_conv1d_w, L0_attn_conv1d_b, L0_attn_x_proj_w, L0_attn_dt_proj_w, L0_attn_dt_proj_b, L0_attn_A_log, L0_attn_D_param, L0_attn_out_proj_w), axis=-1)
    x = _layernorm(x + _L0_ffn_ref(x, L0_ffn_gate_w, L0_ffn_ln_w, L0_ffn_ln_b, L0_ffn_fc1s, L0_ffn_b1s, L0_ffn_fc2s, L0_ffn_b2s), axis=-1)
    return x

_drawn_inputs = setup_inputs


def setup_inputs(seed=0):
    import zlib

    import numpy as np

    out = dict(_drawn_inputs(seed))
    spreads = {'L0_attn_D_param': (1.0, 0.2), 'L0_ffn_ln_w': (1.0, 0.6), 'L0_ffn_ln_b': (0.0, 0.8)}
    factors = {'L0_ffn_b1s': 8.0, 'L0_ffn_b2s': 8.0}
    for name, (base, spread) in spreads.items():
        noise = np.random.default_rng([zlib.crc32(name.encode()), seed]).standard_normal(out[name].shape)
        drawn = base * np.exp(spread * noise) if base else spread * noise
        out[name] = jnp.asarray(drawn.astype(out[name].dtype))
    for name, factor in factors.items():
        out[name] = (out[name] * factor).astype(out[name].dtype)
    return out
```

```python
from contextlib import ExitStack

import concourse.bass as bass
from concourse import mybir

F32 = mybir.dt.float32
BF16 = mybir.dt.bfloat16
I32 = mybir.dt.int32
ALU = mybir.AluOpType
ACT = mybir.ActivationFunctionType
AX = mybir.AxisListType
P = 128
CH = 512
NB = CH // P
LN_EPS = 1e-5


class Alloc:

    def __init__(self, nc, ctx):
        self.nc, self.ctx = nc, ctx

    def sb(self, name, shape, dt=F32):
        return self.ctx.enter_context(self.nc.sbuf_tensor(name, shape, dt))

    def ps(self, name, shape, dt=F32):
        return self.ctx.enter_context(self.nc.psum_tensor(name, shape, dt))

    def sem(self, name):
        return self.ctx.enter_context(self.nc.semaphore(name))


STEPS = [(0, "X", 0), (0, "X", 1), (1, "Y", 0), (1, "X", 2), (1, "X", 3), (2, "Y", 1), (2, "C", 0),
         (3, "Y", 2), (3, "C", 1), (4, "Y", 3), (4, "C", 2), (5, "C", 3), (6, "T", 0), (6, "T", 1),
         (7, "XP", 0), (8, "CT", 0), (8, "D", 0), (8, "D", 1), (9, "D", 2), (9, "D", 3), (9, "L", 0),
         (10, "Z", 0), (10, "Z", 1), (11, "Z", 2), (11, "Z", 3), (12, "O", 0), (13, "O", 1)]
SPARE = 3
GROUP = {"X": "front", "C": "front", "XP": "front", "CT": "front", "D": "front", "Z": "front",
         "Y": "post1", "O": "post1", "T": "post2", "L": "post2"}
BANK = {(kind, i): n % SPARE for n, (_, kind, i) in enumerate(STEPS)}
ORDER = {g: [(k, i) for _, k, i in STEPS if GROUP[k] == g] for g in ("front", "post1", "post2")}
N_FRONT, N_POST1 = len(ORDER["front"]), len(ORDER["post1"])
LAG = {"front": -1, "post1": 1, "post2": 2}


DU = [("delta", 0), ("delta", 1), ("du", 0), ("delta", 2), ("du", 1), ("delta", 3), ("du", 2), ("du", 3)]
DU_AT = {13: (0, 1, 2), 14: (3, 4, 5), 15: (6, 7)}
GATE_AT = 4
SILU_AT, SOFTPLUS_AT, DOUBLE_AT, ROUTER_EXP_AT = 7, 11, 5, 13
NORM_AT, ROUTER_AT, ROUTER_END_AT, STATS_AT = 3, 11, 14, 15


def steps_of(groups):
    return [(slot, kind, i) for slot, kind, i in STEPS if GROUP[kind] in groups]


def nth(kind, i):
    return ORDER[GROUP[kind]].index((kind, i)) + 1


def stage1(nc, d, n_chunks, per_batch):
    DT, NS = 4, 16
    FR, P1, P2 = "front", "post1", "post2"
    BS = 4
    SM = 5
    assert per_batch % 4 == 0
    with ExitStack() as ctx:
        a = Alloc(nc, ctx)
        ident = a.sb("ident", [P, P])
        win = a.sb("win", [P, 2, 1024])
        wconv = a.sb("wconv", [P, DT, 4])
        conv = a.sb("conv", [P, DT, 4, P])
        wx = a.sb("wx", [P, DT, 48])
        wdt = a.sb("wdt", [16, 512])
        wo = a.sb("wo", [P, DT, 256])
        gate = a.sb("gate", [P, 2, 8])
        vecs = a.sb("vecs", [P, 3, DT])
        negA = a.sb("negA", [P, DT, NS])
        half = a.sb("half", [P, NB])
        keep_h = a.sb("keep_h", [P, 1], I32)
        keep_x = a.sb("keep_x", [P, 1], I32)
        xin = a.sb("xin", [P, 2, CH])
        xh = a.sb("xh", [P, DT, 3 + CH])
        u = [a.sb(f"u{i}", [P, DT, CH]) for i in range(2)]
        dl = [a.sb(f"dl{i}", [P, DT, CH]) for i in range(2)]
        du = [a.sb(f"du{i}", [P, DT, CH]) for i in range(2)]
        sz = [a.sb(f"sz{i}", [P, DT, CH]) for i in range(2)]
        xdbl = a.sb("xdbl", [48, CH])
        ct = [a.sb(f"ct{i}", [P, NB, NS]) for i in range(2)]
        bb = [a.sb(f"bb{i}", [P, BS, CH]) for i in range(2)]
        dbu = [a.sb(f"dbu{i}", [P, DT, CH]) for i in range(2)]
        h = [a.sb(f"h{i}", [P, DT, CH]) for i in range(2)]
        hlast = a.sb("hlast", [P, NS, DT])
        carry = a.sb("carry", [P, NS, DT])
        acc = [a.sb(f"acc{i}", [P, NB, 512]) for i in range(2)]
        g = a.sb("g", [P, DT, CH])
        xres = a.sb("xres", [P, NB, 256])
        stats = a.sb("stats", [P, NB, 6])
        mv = a.sb("mv", [P, NB, 2])
        ve = a.sb("ve", [P, NB])
        rstd = a.sb("rstd", [P, NB])
        x2 = a.sb("x2", [P, NB, 256])
        x1t = x2[:].rearrange("p (i b) f -> p i (b f)", i=2)
        lg = a.sb("lg", [P, NB, 8])
        mx = a.sb("mx", [P, NB])
        ssum = a.sb("ssum", [P, NB])
        da = [a.ps("da0", [P, CH])] + [a.sb(f"da{i}", [P, CH]) for i in range(1, DT)]
        ht = [a.ps(f"ht{i}", [P, 512]) for i in range(NB)]
        spare = [a.ps(f"spare{i}", [P, 512]) for i in range(SPARE)]

        S = a.sem
        te_passed, dve_passed, sp_passed = S("te_passed"), S("dve_passed"), S("sp_passed")
        loaded, ident_ok = S("weights_loaded"), S("ident_ready")
        set_ok, negA_ok, conv_ok = S("constants_set"), S("negA_ready"), S("conv_ready")
        exp_done, dbu_done, scan_done, tr_done, mac_done = (
            S("exp_done"), S("dbu_done"), S("scan_done"), S("turned"), S("mac_done"))
        last_saved, carry_ok, halo_ok = S("last_saved"), S("carry_ready"), S("halo_ready")
        keep_h_ok, keep_x_ok = S("keep_h_toggled"), S("keep_x_toggled")
        pe = {FR: S("pe_front"), P1: S("pe_post1"), P2: S("pe_post2")}
        out_of = {FR: S("front_evacuated"), P1: S("post1_evacuated"), P2: S("post2_evacuated")}
        silu_u, silu_z, soft = S("silu_u"), S("silu_z"), S("softplus_steps")
        du_ok, gated, var_ok, rstd_ok = S("du_steps"), S("gated"), S("variance_ready"), S("rstd_ready")
        stats_ok, normed, doubled = S("stats_steps"), S("x1_ready"), S("x1_doubled")
        exp_l, sm = S("router_exp"), S("router_steps")
        xin_in, xres_in, b_out, b_in = (
            S("xin_in"), S("xres_in"), S("b_out"), [S(f"b_in{i}") for i in range(2)])
        x1_out, x2_out = S("x1_out"), S("x2_out")

        def step_done(kind, i, c):
            grp = GROUP[kind]
            k = c - LAG[grp]
            if kind == "L":
                return sm, k * SM + 2
            per = {FR: N_FRONT, P1: N_POST1, P2: 2}[grp]
            return out_of[grp], k * per + nth(kind, i)

        def pe_done(kind, i, c):
            grp = GROUP[kind]
            return pe[grp], (c - LAG[grp]) * len(ORDER[grp]) + nth(kind, i)

        with nc.Block() as block:

            @block.sync
            def _(sp):
                for dst, src in ((win, d["win"]), (wconv, d["wconv"]), (wx, d["wx"]), (wdt, d["wdt"]),
                                 (wo, d["wo"]), (gate, d["gate"]), (vecs, d["vecs"]), (negA, d["alog"])):
                    sp.dma_start(dst[:], src).then_inc(loaded, 16)

                def load_xin(f):
                    sp.dma_start(xin[:], d["xt"][:, bass.ds(f * CH, CH)].rearrange("(k p) t -> p k t", p=P)
                                 ).then_inc(xin_in, 16)

                def b_write(f, q):
                    s, v = step_done("XP", 0, f - 1)
                    sp.wait_ge(s, v)
                    sp.dma_start(d["b_rows"][q], xdbl[16:32, :]).then_inc(b_out, 16)

                def b_read(f, q, part):
                    if part == 0:
                        sp.wait_ge(b_out, 16 * f + 16)
                        sp.sem_inc(sp_passed, 1)
                    if not (isinstance(f, int) and f == 0 and part < 2):
                        sp.wait_ge(dbu_done, f * NS + (part - 1) * BS)
                    sp.dma_start(bb[part % 2][:], d["b_rows"][q, BS * part:BS * part + BS, :].partition_broadcast(P)
                                 ).then_inc(b_in[part % 2], 16)

                def chunk(c, q, groups, more, scan=True):
                    if scan:
                        b_read(c, q, 2)
                    if P2 in groups:
                        sp.wait_ge(normed, c - 1)
                        sp.dma_start(rows(d["x1s"], c - 2)[:, :, 0:256], xres[:]).then_inc(x1_out, 16)
                        sp.wait_ge(doubled, c - 1)
                        sp.dma_start(rows(d["acc"], c - 2), x2[:]).then_inc(x2_out, 16)
                    if P1 in groups:
                        if P2 in groups:
                            s, v = pe_done("T", 1, c)
                            sp.wait_ge(s, v)
                            sp.sem_inc(sp_passed, 1)
                            sp.wait_ge(x1_out, 16 * (c - 1))
                        sp.dma_start(xres[:], rows(d["x"], c - 1)).then_inc(xres_in, 16)
                    if scan:
                        b_read(c, q, 3)
                    if FR in groups:
                        b_write(c + 1, 1 - q)
                        b_read(c + 1, 1 - q, 0)
                        if more:
                            s, v = pe_done("Z", 3, c)
                            sp.wait_ge(s, v)
                            load_xin(c + 2)
                        b_read(c + 1, 1 - q, 1)

                def rows(t, c):
                    return t[bass.ds(c * CH, CH), :].rearrange("(b p) f -> p b f", p=P)

                load_xin(0)
                b_write(0, 0)
                b_read(0, 0, 0)
                b_read(0, 0, 1)
                s, v = pe_done("Z", 3, -1)
                sp.wait_ge(s, v)
                load_xin(1)
                chunk(0, 0, (FR,), True)
                chunk(1, 1, (FR, P1), True)
                with sp.Fori(1, n_chunks // 2 - 1) as j:
                    chunk(2 * j, 0, (FR, P1, P2), True)
                    chunk(2 * j + 1, 1, (FR, P1, P2), True)
                chunk(n_chunks - 2, 0, (FR, P1, P2), False)
                chunk(n_chunks - 1, 1, (P1, P2), False)
                chunk(n_chunks, 0, (P1, P2), False, False)
                chunk(n_chunks + 1, 1, (P2,), False, False)
                sp.wait_ge(x1_out, 16 * n_chunks)
                sp.wait_ge(x2_out, 16 * n_chunks)

            @block.gpsimd
            def _(pool):
                pool.memset(ident[:], 0.0).then_inc(ident_ok, 1)
                pool.memset(half[:], -0.5).then_inc(set_ok, 1)
                pool.memset(keep_h[:], -1).then_inc(keep_h_ok, 1)
                pool.memset(keep_x[:], -1).then_inc(keep_x_ok, 1)
                pool.wait_ge(ident_ok, 1)
                pool.affine_select(out=ident[:], in_=ident[:], compare_op=ALU.not_equal, fill=1.0, base=0,
                                   pattern=[[-1, P]], channel_multiplier=1).then_inc(ident_ok, 1)

                def delta_u(f, q, pieces):
                    for k in pieces:
                        what, dt = DU[k]
                        if k == 0:
                            pool.wait_ge(soft, 2 * f + 2)
                        if what == "delta":
                            pool.tensor_tensor(dl[q][:, dt, :], dl[q][:, dt, :], du[q][:, dt, :],
                                               ALU.add).then_inc(du_ok, 1)
                        else:
                            pool.wait_ge(du_ok, f * len(DU) + DU.index(("delta", dt)) + 1)
                            pool.tensor_tensor(du[q][:, dt, :], dl[q][:, dt, :], u[q][:, dt, :],
                                               ALU.mult).then_inc(du_ok, 1)

                def gating(c, q, i):
                    s, v = step_done("Y", i, c)
                    pool.wait_ge(s, v)
                    if i == 0:
                        pool.wait_ge(silu_z, c)
                    pool.tensor_tensor(g[:, i, :], g[:, i, :], sz[q][:, i, :], ALU.mult).then_inc(gated, 1)

                def chunk(c, q, groups, scan=True):
                    for n in range(NS if scan else 1):
                        if scan:
                            if n == 0:
                                pool.wait_ge(du_ok, (c + 1) * len(DU))
                            part, m = divmod(n, BS)
                            if m == 0:
                                pool.wait_ge(b_in[part % 2], 16 * (c * (NS // BS // 2) + part // 2) + 16)
                            if not (isinstance(c, int) and c == 0 and n < 2):
                                pool.wait_ge(scan_done, (c * NS + n - 1) * DT)
                            pool.tensor_tensor(dbu[n % 2][:], du[q][:],
                                               bb[part % 2][:, m:m + 1, :].to_broadcast([P, DT, CH]),
                                               ALU.mult).then_inc(dbu_done, 1)
                        if P2 in groups and n == (1 if scan else 0):
                            pool.wait_ge(var_ok, c - 1)
                            pool.tensor_tensor(rstd[:], ve[:], half[:], ALU.pow).then_inc(rstd_ok, 1)
                        if P1 in groups:
                            for i in range(DT):
                                if n == GATE_AT + i or not scan:
                                    gating(c, 1 - q, i)
                        if FR in groups and n in DU_AT:
                            delta_u(c + 1, 1 - q, DU_AT[n])

                delta_u(0, 0, range(len(DU)))
                chunk(0, 0, (FR,))
                chunk(1, 1, (FR, P1))
                with pool.Fori(1, n_chunks // 2 - 1) as j:
                    chunk(2 * j, 0, (FR, P1, P2))
                    chunk(2 * j + 1, 1, (FR, P1, P2))
                chunk(n_chunks - 2, 0, (FR, P1, P2))
                chunk(n_chunks - 1, 1, (P1, P2))
                chunk(n_chunks, 0, (P1, P2), False)
                chunk(n_chunks + 1, 1, (P2,), False)

            @block.scalar
            def _(act):
                act.wait_ge(loaded, 16 * 8)
                act.activation(negA[:], negA[:], ACT.Exp).then_inc(negA_ok, 1)
                act.wait_ge(negA_ok, 1)
                act.mul(negA[:], negA[:], -1.0).then_inc(negA_ok, 1)
                act.wait_ge(negA_ok, 2)

                def exps(c, q, n, dts):
                    for dt in dts:
                        e = (c * NS + n) * DT + dt
                        if n == 0:
                            act.wait_ge(du_ok, c * len(DU) + DU.index(("delta", dt)) + 1)
                        if not (isinstance(c, int) and c == 0 and n == 0):
                            act.wait_ge(scan_done, e - DT + 1)
                        act.activation(da[dt][:], dl[q][:, dt, :], ACT.Exp,
                                       scale=negA[:, dt, n:n + 1]).then_inc(exp_done, 1)

                def evacuate(kind, i, c, q):
                    bank = spare[BANK[kind, i]]
                    s, v = pe_done(kind, i, c)
                    act.wait_ge(s, v)
                    done = out_of[GROUP[kind]]
                    f = c + 1
                    if kind == "X":
                        if i == 0:
                            act.wait_ge(halo_ok, f + 1)
                        act.copy(xh[:, i, 3:], bank[:]).then_inc(done, 1)
                    elif kind == "C":
                        if not (isinstance(c, int) and c < 1):
                            s, v = step_done("Y", i, c)
                            act.wait_ge(s, v)
                        act.activation(u[q][:, i, :], bank[:], ACT.Identity,
                                       bias=vecs[:, 0, i:i + 1]).then_inc(done, 1)
                    elif kind == "Z":
                        if i == 0 and not (isinstance(c, int) and c < 1):
                            act.wait_ge(gated, DT * c)
                        act.copy(sz[q][:, i, :], bank[:]).then_inc(done, 1)
                    elif kind == "XP":
                        if not (isinstance(f, int) and f == 0):
                            act.wait_ge(b_out, 16 * f)
                        act.copy(xdbl[:], bank[0:48, :]).then_inc(done, 1)
                    elif kind == "CT":
                        act.copy(ct[q][:], bank[:, 0:NB * 48].rearrange("p (b r) -> p b r", b=NB)[:, :, 32:48]
                                 ).then_inc(done, 1)
                    elif kind == "D":
                        if not (isinstance(f, int) and f < 2):
                            act.wait_ge(dbu_done, (f - 1) * NS)
                        act.activation(dl[q][:, i, :], bank[:], ACT.Abs, bias=vecs[:, 1, i:i + 1])
                        act.activation(du[q][:, i, :], bank[:], ACT.Relu,
                                       bias=vecs[:, 1, i:i + 1]).then_inc(done, 1)
                    elif kind == "T":
                        if i == 0:
                            act.wait_ge(x2_out, 16 * (c - 1))
                        act.copy(x1t[:, i, :], bank[:]).then_inc(done, 1)

                def silu_of_u(f, q):
                    s, v = step_done("C", 3, f - 1)
                    act.wait_ge(s, v)
                    act.activation(u[q][:], u[q][:], ACT.Silu).then_inc(silu_u, 1)

                def silu_of_z(c, q):
                    s, v = step_done("Z", 3, c - 1)
                    act.wait_ge(s, v)
                    act.activation(sz[q][:], sz[q][:], ACT.Silu).then_inc(silu_z, 1)

                def softplus(f, q):
                    s, v = step_done("D", 3, f - 1)
                    act.wait_ge(s, v)
                    act.activation(dl[q][:], dl[q][:], ACT.Exp, scale=-1.0).then_inc(soft, 1)
                    act.wait_ge(soft, 2 * f + 1)
                    act.activation(dl[q][:], dl[q][:], ACT.Ln, bias=1.0).then_inc(soft, 1)

                def chunk(c, q, groups, scan=True):
                    todo = steps_of(groups)
                    for n in range(NS + 2):
                        if scan and n < NS:
                            exps(c, q, n, range(DT))
                        for slot, kind, i in todo:
                            if slot == n - 2 and kind not in ("Y", "O", "L"):
                                evacuate(kind, i, c, 1 - q)
                        if n == SILU_AT:
                            if FR in groups:
                                silu_of_u(c + 1, 1 - q)
                            if scan:
                                silu_of_z(c, q)
                        if n == SOFTPLUS_AT and FR in groups:
                            softplus(c + 1, 1 - q)
                        if n == DOUBLE_AT and P2 in groups:
                            act.wait_ge(normed, c - 1)
                            act.mul(x2[:], xres[:], 2.0).then_inc(doubled, 1)
                        if n == ROUTER_EXP_AT and P2 in groups:
                            act.wait_ge(sm, (c - 2) * SM + 2)
                            act.activation(lg[:], lg[:], ACT.Exp).then_inc(exp_l, 1)

                for _, kind, i in steps_of((FR,)):
                    if (kind, i) == ("XP", 0):
                        silu_of_u(0, 0)
                    evacuate(kind, i, -1, 0)
                    if (kind, i) == ("D", 3):
                        softplus(0, 0)
                chunk(0, 0, (FR,))
                chunk(1, 1, (FR, P1))
                with act.Fori(1, n_chunks // 2 - 1) as j:
                    chunk(2 * j, 0, (FR, P1, P2))
                    chunk(2 * j + 1, 1, (FR, P1, P2))
                chunk(n_chunks - 2, 0, (FR, P1, P2))
                chunk(n_chunks - 1, 1, (P1, P2))
                chunk(n_chunks, 0, (P1, P2), False)
                chunk(n_chunks + 1, 1, (P2,), False)

            @block.tensor
            def _(te):
                te.wait_ge(loaded, 16 * 8)
                te.wait_ge(ident_ok, 2)
                te.wait_ge(conv_ok, 1)

                def step(kind, i, c, q, prev):
                    bank = spare[BANK[kind, i]]
                    if prev:
                        s, v = step_done(*prev)
                        te.wait_ge(s, v)
                    f, p = c + 1, c - 1
                    done = pe[GROUP[kind]]
                    if kind in ("X", "Z"):
                        if kind == "X" and i == 0:
                            te.wait_ge(xin_in, 16 * f + 16)
                        col = (512 if kind == "Z" else 0) + i * P
                        for k in range(2):
                            last = te.matmul(bank[:], win[:, k, col:col + P], xin[:, k, :],
                                             start=k == 0, stop=k == 1)
                    elif kind == "C":
                        s, v = step_done("X", i, c)
                        te.wait_ge(s, v)
                        for k in range(4):
                            last = te.matmul(bank[:], conv[:, i, k, :], xh[:, i, k:k + CH],
                                             start=k == 0, stop=k == 3)
                    elif kind == "XP":
                        te.wait_ge(silu_u, f + 1)
                        for k in range(DT):
                            last = te.matmul(bank[0:48, :], wx[:, k, :], u[q][:, k, :],
                                             start=k == 0, stop=k == DT - 1)
                    elif kind == "CT":
                        s, v = step_done("XP", 0, c)
                        te.wait_ge(s, v)
                        te.sem_inc(te_passed, 1)
                        for b in range(NB):
                            last = te.transpose(bank[:, b * 48:b * 48 + 48], xdbl[:, b * P:(b + 1) * P],
                                                ident[0:48, 0:48])
                    elif kind == "D":
                        last = te.matmul(bank[:], wdt[:, i * P:(i + 1) * P], xdbl[0:16, :],
                                         start=True, stop=True)
                    elif kind == "Y":
                        if i == 0:
                            te.wait_ge(mac_done, c * NS * NB)
                        for b in range(NB):
                            last = te.transpose(bank[:, b * P:(b + 1) * P], acc[q][:, b, i * P:(i + 1) * P],
                                                ident[:])
                    elif kind == "O":
                        if i == 0:
                            te.wait_ge(gated, DT * (p + 1))
                        for b in range(2):
                            for k in range(DT):
                                t0 = (2 * i + b) * P
                                last = te.matmul(bank[:, b * 256:(b + 1) * 256], g[:, k, t0:t0 + P], wo[:, k, :],
                                                 start=k == 0, stop=k == DT - 1)
                    elif kind == "T":
                        if i == 0:
                            te.wait_ge(normed, c - 1)
                        for b in range(2):
                            for k in range(2):
                                last = te.transpose(bank[:, (2 * b + k) * P:(2 * b + k + 1) * P],
                                                    xres[:, 2 * i + b, k * P:(k + 1) * P], ident[:])
                    elif kind == "L":
                        s, v = step_done("T", 1, c)
                        te.wait_ge(s, v)
                        for b in range(NB):
                            for k in range(2):
                                o = (2 * (b % 2) + k) * P
                                last = te.matmul(bank[:, b * 8:b * 8 + 8], x1t[:, b // 2, o:o + P], gate[:, k, :],
                                                 start=k == 0, stop=k == 1)
                    last.then_inc(done, 1)

                def chunk(c, q, groups, before, scan=True):
                    todo, used = steps_of(groups), steps_of(before)
                    for n in range(NS):
                        if scan:
                            unit = c * NS + n
                            te.wait_ge(scan_done, unit * DT + DT)
                            for b in range(NB):
                                if not (isinstance(c, int) and c == 0 and n == 0):
                                    te.wait_ge(mac_done, (unit - 1) * NB + b + 1)
                                for dt in range(DT):
                                    last = te.transpose(ht[b][:, dt * P:(dt + 1) * P],
                                                        h[n % 2][:, dt, b * P:(b + 1) * P], ident[:])
                                last.then_inc(tr_done, 1)
                        for k, (slot, kind, i) in enumerate(todo):
                            if slot != n:
                                continue
                            same = [(x, y, c) for _, x, y in todo[:k] if BANK[x, y] == BANK[kind, i]]
                            wrap = [(x, y, c - 1) for _, x, y in used if BANK[x, y] == BANK[kind, i]]
                            prev = (same or wrap or [None])[-1]
                            step(kind, i, c, 1 - q, prev)

                prev_of = {}
                for _, kind, i in steps_of((FR,)):
                    step(kind, i, -1, 0, prev_of.get(BANK[kind, i]))
                    prev_of[BANK[kind, i]] = (kind, i, -1)
                chunk(0, 0, (FR,), (FR,))
                chunk(1, 1, (FR, P1), (FR,))
                with te.Fori(1, n_chunks // 2 - 1) as j:
                    chunk(2 * j, 0, (FR, P1, P2), (FR, P1, P2))
                    chunk(2 * j + 1, 1, (FR, P1, P2), (FR, P1, P2))
                chunk(n_chunks - 2, 0, (FR, P1, P2), (FR, P1, P2))
                chunk(n_chunks - 1, 1, (P1, P2), (FR, P1, P2))
                chunk(n_chunks, 0, (P1, P2), (P1, P2), False)
                chunk(n_chunks + 1, 1, (P2,), (P1, P2), False)

            @block.vector
            def _(dve):
                dve.wait_ge(loaded, 16 * 8)
                dve.wait_ge(ident_ok, 2)
                for dt in range(DT):
                    for k in range(4):
                        last = dve.tensor_scalar(conv[:, dt, k, :], ident[:], wconv[:, dt, k:k + 1], None, ALU.mult)
                last.then_inc(conv_ok, 1)
                dve.memset(xh[:, :, 0:3], 0.0).then_inc(halo_ok, 1)

                def scans(c, q, n):
                    unit = c * NS + n
                    first = isinstance(c, int) and c == 0
                    dve.wait_ge(dbu_done, unit + 1)
                    if not (first and n < 2):
                        dve.wait_ge(tr_done, (unit - 1) * NB)
                        dve.wait_ge(last_saved, unit - 1)
                    for dt in range(DT):
                        dve.wait_ge(exp_done, unit * DT + dt + 1)
                        start = 0.0 if first else (carry if q == 0 else hlast)[:, n, dt:dt + 1]
                        dve.tensor_tensor_scan(h[n % 2][:, dt, :], da[dt][:], dbu[n % 2][:, dt, :], start,
                                              ALU.mult, ALU.add).then_inc(scan_done, 1)
                    dve.wait_ge(scan_done, unit * DT + DT)
                    dve.tensor_copy(hlast[:, n, :], h[n % 2][:, :, CH - 1]).then_inc(last_saved, 1)

                def macs(c, q, n):
                    unit = c * NS + n
                    for b in range(NB):
                        dve.wait_ge(tr_done, unit * NB + b + 1)
                        cc = ct[q][:, b, n:n + 1]
                        if n == 0:
                            if b == 0:
                                s, v = step_done("CT", 0, c - 1)
                                dve.wait_ge(s, v)
                                if not (isinstance(c, int) and c < 2):
                                    dve.wait_ge(pe[P1], (c - 2) * N_POST1 + nth("Y", 3))
                            ins = dve.tensor_scalar(acc[q][:, b, :], ht[b][:], cc, None, ALU.mult)
                        else:
                            dve.wait_ge(mac_done, (unit - 1) * NB + b + 1)
                            ins = dve.scalar_tensor_tensor(acc[q][:, b, :], ht[b][:], cc, acc[q][:, b, :],
                                                          ALU.mult, ALU.add)
                        ins.then_inc(mac_done, 1)

                def post1_step(kind, i, c, q):
                    p = c - 1
                    bank = spare[BANK[kind, i]]
                    s, v = pe_done(kind, i, c)
                    dve.wait_ge(s, v)
                    if kind == "Y":
                        if i == 0 and not (isinstance(c, int) and c == 1):
                            dve.wait_ge(pe[P1], (p - 1) * N_POST1 + nth("O", 1))
                        dve.scalar_tensor_tensor(g[:, i, :], u[q][:, i, :], vecs[:, 2, i:i + 1], bank[:],
                                                ALU.mult, ALU.add).then_inc(out_of[P1], 1)
                    else:
                        if i == 0:
                            dve.wait_ge(xres_in, 16 * c)
                        x = xres[:, 2 * i:2 * i + 2, :].rearrange("p b f -> p (b f)")
                        dve.tensor_tensor(x, bank[:], x, ALU.add).then_inc(out_of[P1], 1)

                def layer_stats(c):
                    p = c - 1
                    s, v = step_done("O", 1, c)
                    dve.wait_ge(s, v)
                    if not (isinstance(c, int) and c == 1):
                        dve.wait_ge(rstd_ok, p)
                    for b in range(NB):
                        last = dve.bn_stats(stats[:, b, :], xres[:, b, :])
                    last.then_inc(stats_ok, 1)
                    dve.wait_ge(stats_ok, 2 * p + 1)
                    dve.sem_inc(dve_passed, 1)
                    for b in range(NB):
                        last = dve.bn_aggr(mv[:, b, :], stats[:, b, :])
                    last.then_inc(stats_ok, 1)
                    dve.wait_ge(stats_ok, 2 * p + 2)
                    dve.tensor_scalar(ve[:], mv[:, :, 1], LN_EPS, None, ALU.add).then_inc(var_ok, 1)

                def normalise(c):
                    r = c - 2
                    dve.wait_ge(rstd_ok, r + 1)
                    for b in range(NB):
                        last = dve.tensor_scalar(xres[:, b, :], xres[:, b, :], mv[:, b, 0:1], rstd[:, b:b + 1],
                                                ALU.subtract, ALU.mult)
                    last.then_inc(normed, 1)

                def router(c, part):
                    r = c - 2
                    if part == 0:
                        s, v = pe_done("L", 0, c)
                        dve.wait_ge(s, v)
                        bank = spare[BANK["L", 0]][:, 0:NB * 8].rearrange("p (b e) -> p b e", b=NB)
                        dve.reduce_max(mx[:], bank, AX.X).then_inc(sm, 1)
                        dve.wait_ge(sm, r * SM + 1)
                        ins = dve.tensor_tensor(lg[:], bank, mx[:].unsqueeze(2).to_broadcast([P, NB, 8]), ALU.subtract)
                        ins.then_inc(sm, 1)
                    else:
                        dve.wait_ge(exp_l, r + 1)
                        dve.reduce_sum(ssum[:], lg[:], AX.X).then_inc(sm, 1)
                        dve.wait_ge(sm, r * SM + 3)
                        dve.reciprocal(ssum[:], ssum[:]).then_inc(sm, 1)
                        dve.wait_ge(sm, r * SM + 4)
                        dve.tensor_tensor(d["scores"][:, bass.ds(r * NB, NB), :], lg[:],
                                         ssum[:].unsqueeze(2).to_broadcast([P, NB, 8]), ALU.mult).then_inc(sm, 1)

                def chunk(c, q, groups, j, scan=True):
                    first = isinstance(c, int) and c == 0
                    todo = [(s, k, i) for s, k, i in steps_of(groups) if k in ("Y", "O")]
                    if scan and q == 0 and not first:
                        dve.wait_ge(last_saved, c * NS)
                        dve.wait_ge(keep_h_ok, j)
                        dve.tensor_scalar(carry[:].rearrange("p n d -> p (n d)").bitcast(I32),
                                         hlast[:].rearrange("p n d -> p (n d)").bitcast(I32),
                                         keep_h[:, 0:1], None, ALU.bitwise_and).then_inc(carry_ok, 1)
                        dve.wait_ge(carry_ok, j)
                        dve.tensor_scalar(keep_h[:], keep_h[:], -1, None, ALU.bitwise_xor).then_inc(keep_h_ok, 1)
                    for n in range(NS):
                        if scan:
                            scans(c, q, n)
                            if n == 0 and FR in groups:
                                halo(c + 1, 1 - q, j)
                            if n > 0:
                                macs(c, q, n - 1)
                        if n == 0 and not first and (scan or P1 in groups and P2 in groups):
                            macs(c - 1, 1 - q, NS - 1)
                        for slot, kind, i in todo:
                            if slot + (1 if scan else 0) == n:
                                post1_step(kind, i, c, 1 - q)
                        if P2 in groups and n == NORM_AT:
                            normalise(c)
                        if P2 in groups and n == ROUTER_AT:
                            router(c, 0)
                        if P2 in groups and n == ROUTER_END_AT:
                            router(c, 1)
                        if P1 in groups and n == STATS_AT:
                            layer_stats(c)

                def halo(f, q, j):
                    s, v = pe_done("C", 3, f - 2)
                    dve.wait_ge(s, v)
                    dst, src = xh[:, :, 0:3], xh[:, :, CH:CH + 3]
                    if q == 1:
                        dve.tensor_copy(dst, src).then_inc(halo_ok, 1)
                    else:
                        dve.wait_ge(keep_x_ok, j + 1)
                        dve.tensor_scalar(dst.bitcast(I32), src.bitcast(I32), keep_x[:, 0:1], None,
                                         ALU.bitwise_and).then_inc(halo_ok, 1)
                        dve.wait_ge(halo_ok, f + 1)
                        dve.tensor_scalar(keep_x[:], keep_x[:], -1, None, ALU.bitwise_xor).then_inc(keep_x_ok, 1)

                chunk(0, 0, (FR,), 0)
                chunk(1, 1, (FR, P1), 0)
                with dve.Fori(1, n_chunks // 2 - 1) as j:
                    chunk(2 * j, 0, (FR, P1, P2), j)
                    chunk(2 * j + 1, 1, (FR, P1, P2), j)
                last_pair = n_chunks // 2 - 1
                chunk(n_chunks - 2, 0, (FR, P1, P2), last_pair)
                chunk(n_chunks - 1, 1, (P1, P2), last_pair)
                chunk(n_chunks, 0, (P1, P2), last_pair + 1, False)
                chunk(n_chunks + 1, 1, (P2,), last_pair + 1, False)


def stage2(nc, d, n_tok):
    E, G = 8, 16
    SL = n_tok // (G * P)
    J = SL * P
    K = n_tok // E
    BITS = 30
    with ExitStack() as ctx:
        a = Alloc(nc, ctx)
        ident = a.sb("ident2", [P, P])
        same = a.sb("same_expert", [P, P])
        before = a.sb("groups_before", [P, P])
        ones = a.sb("ones", [P, J])
        sc = a.sb("sc", [P, J])
        gt = a.sb("gt", [P, J])
        eq = a.sb("eq", [P, J])
        run = a.sb("run", [P, J])
        pos = a.sb("pos", [P, J])
        slot = a.sb("slot", [P, J], I32)
        part = a.sb("part", [P, J], I32)
        thr = a.sb("thr", [P, 1], I32)
        bit = a.sb("bit", [P, 1], I32)
        cand = a.sb("cand", [P, 1], I32)
        take = a.sb("take", [P, 1], I32)
        cnt = a.sb("cnt", [P, 1])
        lim = a.sb("lim", [P, 1])
        off = a.sb("off", [P, 1])
        big = [a.ps(f"big{i}", [P, 512]) for i in range(2)]
        tot = a.ps("tot", [P, 4])
        made, const_ok, mats = a.sem("masks_made"), a.sem("constants2"), a.sem("masks_ready")
        counted_take = a.sem("count_compared")
        turned, sc_ok, counted, summed, step = (
            a.sem("scores_turned"), a.sem("scores_ready"), a.sem("counted"), a.sem("summed"), a.sem("bisect_step"))
        chain, sums, back = a.sem("select_step"), a.sem("select_sums"), a.sem("slots_turned")
        passed = a.sem("passed2")
        packed_ok = a.sem("scores_packed")
        packed = a.sb("packed", [P, SL, E * G])
        stored = a.sem("scores_stored")
        view = d["scores"].rearrange("p (g s) e -> p s e g", s=SL)
        with nc.Block() as block:

            @block.sync
            def _(sp):
                sp.dma_start(d["x1s"][:, 256:264].rearrange("(b p) e -> p b e", p=P), d["scores"]).then_inc(stored, 16)
                sp.wait_ge(stored, 16)

            @block.gpsimd
            def _(pool):
                for m, v in ((ident, 0.0), (same, 1.0)):
                    pool.memset(m[:], v).then_inc(made, 1)
                pool.memset(ones[:], 1.0).then_inc(const_ok, 1)
                pool.memset(thr[:], 0).then_inc(const_ok, 1)
                pool.memset(bit[:], 1 << (BITS - 1)).then_inc(step, 1)
                pool.wait_ge(made, 2)
                pool.affine_select(out=ident[:], in_=ident[:], compare_op=ALU.not_equal, fill=1.0, base=0,
                                   pattern=[[-1, P]], channel_multiplier=1).then_inc(mats, 1)
                grid = same[:].rearrange("p (e g) -> p e g", e=E)
                pool.affine_select(out=grid, in_=grid, compare_op=ALU.is_ge, fill=0.0, base=0,
                                   pattern=[[-G, E], [0, G]], channel_multiplier=1).then_inc(made, 1)
                pool.wait_ge(made, 3)
                pool.affine_select(out=grid, in_=grid, compare_op=ALU.is_ge, fill=0.0, base=G - 1,
                                   pattern=[[G, E], [0, G]], channel_multiplier=-1).then_inc(made, 1)
                pool.wait_ge(made, 4)
                pool.affine_select(out=before[:], in_=same[:], compare_op=ALU.is_ge, fill=0.0, base=-1,
                                   pattern=[[1, P]], channel_multiplier=-1).then_inc(mats, 1)

            @block.tensor
            def _(te):
                te.wait_ge(mats, 2)
                te.wait_ge(packed_ok, 1)
                for s in range(SL):
                    te.transpose(big[s // 4][:, (s % 4) * P:(s % 4 + 1) * P], packed[:, s, :], ident[:]
                                 ).then_inc(turned, 1)
                with te.Fori(0, BITS) as i:
                    te.wait_ge(counted, i + 1)
                    te.matmul(tot[:, 0:1], same[:], cnt[:], start=True, stop=True).then_inc(summed, 1)
                te.wait_ge(chain, 3)
                te.matmul(tot[:, 1:2], same[:], cnt[:], start=True, stop=True)
                te.matmul(tot[:, 2:3], before[:], run[:, J - 1:J], start=True, stop=True).then_inc(sums, 1)
                te.wait_ge(chain, 8)
                te.matmul(tot[:, 3:4], before[:], pos[:, J - 1:J], start=True, stop=True).then_inc(sums, 1)
                te.wait_ge(chain, 10)
                for s in range(SL):
                    te.transpose(big[s // 4][:, (s % 4) * P:(s % 4 + 1) * P], run[:, s * P:(s + 1) * P], ident[:]
                                 ).then_inc(back, 1)

            @block.vector
            def _(dve):
                dve.wait_ge(const_ok, 2)
                dve.tensor_copy(packed[:].rearrange("p s (e g) -> p s e g", e=E), view).then_inc(packed_ok, 1)
                dve.wait_ge(turned, SL)
                for s in range(0, SL, 4):
                    dve.tensor_copy(sc[:, s * P:(s + 4) * P], big[s // 4][:]).then_inc(sc_ok, 1)
                dve.wait_ge(sc_ok, (SL + 3) // 4)
                with dve.Fori(0, BITS) as i:
                    dve.wait_ge(step, 3 * i + 1)
                    dve.tensor_tensor(cand[:], thr[:], bit[:], ALU.bitwise_or).then_inc(step, 1)
                    dve.wait_ge(step, 3 * i + 2)
                    dve.tensor_scalar(run[:], sc[:], cand[:].bitcast(F32), 0.0, ALU.is_ge, ALU.add,
                                      accum_out=cnt[:]).then_inc(counted, 1)
                    dve.tensor_scalar(bit[:], bit[:], 1, None, ALU.logical_shift_right).then_inc(step, 1)
                    dve.wait_ge(summed, i + 1)
                    dve.tensor_scalar(take[:], tot[:, 0:1], float(K), None, ALU.is_ge).then_inc(counted_take, 1)
                    dve.wait_ge(counted_take, i + 1)
                    dve.sem_inc(passed, 1)
                    dve.copy_predicated(thr[:], take[:], cand[:]).then_inc(step, 1)
                dve.wait_ge(step, 3 * BITS + 1)
                t = thr[:].bitcast(F32)
                dve.tensor_scalar(gt[:], sc[:], t, 0.0, ALU.is_gt, ALU.add, accum_out=cnt[:]).then_inc(chain, 1)
                dve.tensor_scalar(eq[:], sc[:], t, None, ALU.is_equal).then_inc(chain, 1)
                dve.wait_ge(chain, 2)
                dve.tensor_tensor_scan(run[:], ones[:], eq[:], 0.0, ALU.mult, ALU.add).then_inc(chain, 1)
                dve.wait_ge(sums, 1)
                dve.tensor_scalar(lim[:], tot[:, 1:2], -1.0, float(K), ALU.mult, ALU.add).then_inc(chain, 1)
                dve.wait_ge(chain, 4)
                dve.tensor_tensor(lim[:], lim[:], tot[:, 2:3], ALU.subtract).then_inc(chain, 1)
                dve.wait_ge(chain, 5)
                dve.scalar_tensor_tensor(eq[:], run[:], lim[:], eq[:], ALU.is_le, ALU.mult).then_inc(chain, 1)
                dve.wait_ge(chain, 6)
                dve.tensor_tensor(gt[:], gt[:], eq[:], ALU.add).then_inc(chain, 1)
                dve.wait_ge(chain, 7)
                dve.tensor_tensor_scan(pos[:], ones[:], gt[:], 0.0, ALU.mult, ALU.add).then_inc(chain, 1)
                dve.wait_ge(sums, 2)
                dve.tensor_copy(off[:], tot[:, 3:4]).then_inc(chain, 1)
                dve.wait_ge(chain, 9)
                dve.scalar_tensor_tensor(run[:], pos[:], off[:], gt[:], ALU.add, ALU.mult).then_inc(chain, 1)
                dve.wait_ge(back, SL)
                for s in range(0, SL, 4):
                    last = dve.tensor_scalar(slot[:, s * P:(s + 4) * P], big[s // 4][:], -1.0, None, ALU.add)
                last.then_inc(chain, 1)
                dve.wait_ge(chain, 11)
                dve.tensor_scalar(part[:], slot[:], P - 1, None, ALU.bitwise_and).then_inc(chain, 1)
                dve.tensor_scalar(slot[:], slot[:], 7, None, ALU.arith_shift_right).then_inc(chain, 1)
                dve.wait_ge(chain, 13)
                flat = "p s e g -> p (s e g)"
                dve.tensor_copy(d["lo"].rearrange(flat), part[:]).then_inc(chain, 1)
                dve.tensor_copy(d["hi"].rearrange(flat), slot[:]).then_inc(chain, 1)
                dve.wait_ge(chain, 15)


def stage3(nc, d, n_tok):
    E, G = 8, 16
    SL = n_tok // (G * P)
    K = n_tok // E
    NT = K // P
    NG = NT // 4
    FM = 8
    assert NG == 4 and SL == 8
    with ExitStack() as ctx:
        a = Alloc(nc, ctx)
        ident = a.sb("ident3", [P, P])
        counti = a.sb("counti", [P, P], I32)
        count = a.sb("count", [P, P], BF16)
        blki = a.sb("blki", [P, SL, G], I32)
        blk = a.sb("blk", [P, SL, G], BF16)
        pidi = a.sb("pidi", [P, 1], I32)
        pid = a.sb("pid", [P, 1])
        half = a.sb("half3", [P, 4])
        w1 = [a.sb(f"w1_{i}", [P, 2, 1024]) for i in range(2)]
        w2 = [a.sb(f"w2_{i}", [P, FM, 256]) for i in range(2)]
        b1 = [a.sb(f"b1_{i}", [P, FM]) for i in range(2)]
        b2 = a.sb("b2", [P, E, 256])
        ln = a.sb("ln", [P, 2, 2])
        isin = a.sb("isin", [P, SL, G, 16], BF16)
        rhs = a.sb("rhs", [P, SL, G, 2, 16], BF16)
        onehot = [a.sb(f"onehot{i}", [P, G, P], BF16) for i in range(2)]
        idxf = a.sb("idxf", [P, 16])
        idx = [a.sb(f"idx{i}", [P, NT], I32) for i in range(2)]
        xg = [a.sb(f"xg{i}", [P, 4, 264]) for i in range(4)]
        xn = [a.sb(f"xn{i}", [P, 4, 256]) for i in range(2)]
        stats = a.sb("stats3", [P, 4, 6])
        mv = a.sb("mv3", [P, 4, 2])
        ve = a.sb("ve3", [P, 4])
        rstd = a.sb("rstd3", [P, 4])
        yt = [a.sb(f"yt{i}", [P, 2, 512]) for i in range(2)]
        hb = [a.sb(f"hb{i}", [P, FM, 512]) for i in range(2)]
        ot = [a.sb(f"ot{i}", [P, 4, 256]) for i in range(2)]
        tp = [a.ps(f"tp{i}", [P, 512]) for i in range(2)]
        f1 = [a.ps(f"f1_{i}", [P, 512]) for i in range(2)]
        f2 = [a.ps(f"f2_{i}", [P, 512]) for i in range(2)]
        lists = a.ps("lists", [P, 32])
        S = a.sem
        pool_passed, dve_passed = S("pool_passed3"), S("dve_passed3")
        made, ident_ok, iotas, consts = S("made3"), S("ident3_ready"), S("iotas"), S("constants3")
        small_in, w_in = S("small_in"), [S(f"weights_in{i}") for i in range(2)]
        rhs_ok, oh_ok, oh_used, idx_ok = S("rhs_steps"), S("onehot_ready"), S("onehot_used"), S("idx_ready")
        gathered = [S(f"rows_gathered{t}") for t in range(NG)]
        added = [S(f"rows_added{t}") for t in range(NG)]
        st, var_ok, rstd_ok, xn_ok = S("stats3_steps"), S("variance3"), S("rstd3_ready"), S("xn_ready")
        tp_ok, yt_ok = S("turned3"), S("yt_ready")
        f1_ok, gelu_ok, f2_ok = S("fc1_done"), S("gelu_done"), S("fc2_done")
        idxf_ok = S("idxf_ready")
        biased, ot_ok = S("biased"), S("out_rows_ready")
        with nc.Block() as block:

            def run(eng, prologue, step):
                prologue()
                for p in range(2):
                    for t in range(NG):
                        step(p, t, p, t < 2, 2)
                with eng.Fori(1, E // 2 - 1) as j:
                    for p in range(2):
                        for t in range(NG):
                            step(2 * j + p, t, p, t < 2, 2)
                for p in range(2):
                    for t in range(NG):
                        step(E - 2 + p, t, p, t < 2 and p == 0, min(2, NG - 1 - t) if p else 2)

            @block.sync
            def _(sp):
                sp.dma_start(ln[:], d["ln"]).then_inc(small_in, 16)
                sp.dma_start(b2[:].rearrange("p e f -> p (e f)"), d["b2"].partition_broadcast(P)).then_inc(small_in, 16)

                def load(e, p):
                    sp.dma_start(w1[p][:], d["w1"][bass.ds(e, 1)].rearrange("a p k f -> p (a k) f")).then_inc(w_in[p], 16)
                    sp.dma_start(w2[p][:], d["w2"][bass.ds(e, 1)].rearrange("a p k f -> p (a k) f")).then_inc(w_in[p], 16)
                    sp.dma_start(b1[p][:], d["b1"][bass.ds(e, 1)].rearrange("a p k -> p (a k)")).then_inc(w_in[p], 16)

                def step(e, t, p, lists_, ahead):
                    if t == 0 and not (isinstance(e, int) and e == E - 1):
                        sp.wait_ge(f2_ok, e * NT)
                        load(e + 1, 1 - p)

                run(sp, lambda: load(0, 0), step)

            @block.gpsimd
            def _(pool):
                pool.memset(ident[:], 0.0).then_inc(made, 1)
                pool.memset(half[:], -0.5).then_inc(made, 1)
                pool.wait_ge(made, 2)
                pool.affine_select(out=ident[:], in_=ident[:], compare_op=ALU.not_equal, fill=1.0, base=0,
                                   pattern=[[-1, P]], channel_multiplier=1).then_inc(ident_ok, 1)
                pool.iota(counti[:], [[1, P]], base=0, channel_multiplier=0).then_inc(iotas, 1)
                pool.iota(blki[:], [[1, SL], [SL, G]], base=0, channel_multiplier=0).then_inc(iotas, 1)
                pool.iota(pidi[:], [[0, 1]], base=0, channel_multiplier=1).then_inc(iotas, 1)

                def gather(e, t, p):
                    grp = e * NG + t
                    if t == 0:
                        pool.wait_ge(idx_ok, e + 1)
                    if not isinstance(e, int) or e > 0:
                        pool.wait_ge(ot_ok, grp - 3)
                    pool.sem_inc(pool_passed, 1)
                    for b in range(4):
                        pool.indirect_dma_start(
                            out=xg[t][:, b, :], out_offset=None, in_=d["x1s"],
                            in_offset=bass.IndirectOffsetOnAxis(ap=idx[p][:, 4 * t + b:4 * t + b + 1], axis=0),
                        ).then_inc(gathered[t], 16)

                def power(grp):
                    pool.wait_ge(var_ok, grp + 1)
                    pool.tensor_tensor(rstd[:], ve[:], half[:], ALU.pow).then_inc(rstd_ok, 1)

                def prologue():
                    gather(0, 0, 0)
                    gather(0, 1, 0)
                    power(0)

                def step(e, t, p, lists_, ahead):
                    grp = e * NG + t
                    if ahead >= 2:
                        if t + 2 < NG:
                            gather(e, t + 2, p)
                        else:
                            gather(e + 1, t + 2 - NG, 1 - p)
                    if ahead >= 1:
                        power(grp + 1)
                    pool.wait_ge(ot_ok, grp + 1)
                    if t == 0:
                        for k in range(NG):
                            pool.wait_ge(added[k], 64 * e)
                    pool.sem_inc(pool_passed, 1)
                    for b in range(4):
                        pool.indirect_dma_start(
                            out=d["acc"], out_offset=bass.IndirectOffsetOnAxis(
                                ap=idx[p][:, 4 * t + b:4 * t + b + 1], axis=0),
                            in_=ot[t % 2][:, b, :], in_offset=None, compute_op=ALU.add).then_inc(added[t], 16)

                run(pool, prologue, step)
                for k in range(NG):
                    pool.wait_ge(added[k], 64 * E)

            @block.scalar
            def _(act):
                act.wait_ge(small_in, 32)

                def turn_out(grp, q):
                    for k in range(2):
                        act.wait_ge(tp_ok, 2 * grp + k + 1)
                        act.activation(yt[q][:, k, :], tp[k][:], ACT.Identity, bias=ln[:, 1, k:k + 1],
                                       scale=ln[:, 0, k:k + 1]).then_inc(yt_ok, 1)

                def step(e, t, p, lists_, ahead):
                    grp = e * NG + t
                    if t == 0:
                        act.wait_ge(w_in[p], 24 * (e - p) + 48)
                    for m in range(FM):
                        act.wait_ge(f1_ok, grp * FM + m + 1)
                        if m == 0 and (not isinstance(e, int) or grp >= 2):
                            act.wait_ge(f2_ok, (grp - 1) * 4)
                        act.activation(hb[t % 2][:, m, :], f1[m % 2][:], ACT.Gelu_apprx_tanh,
                                       bias=b1[p][:, m:m + 1]).then_inc(gelu_ok, 1)
                    if ahead >= 1:
                        turn_out(grp + 1, (t + 1) % 2)

                run(act, lambda: turn_out(0, 0), step)

            @block.tensor
            def _(te):
                te.wait_ge(ident_ok, 1)

                def token_list(e, slabs):
                    for s in slabs:
                        te.wait_ge(oh_ok, e * SL + s + 1)
                        if s == 0:
                            te.wait_ge(rhs_ok, 3 * e + 3)
                        for g in range(G):
                            last = te.matmul(lists[:], onehot[s % 2][:, g, :],
                                             rhs[:, s, g].rearrange("p a t -> p (a t)"),
                                             start=s == 0 and g == 0, stop=s == SL - 1 and g == G - 1)
                        last.then_inc(oh_used, 1)

                def turn(grp, q):
                    te.wait_ge(xn_ok, grp + 1)
                    for k in range(2):
                        if not isinstance(grp, int) or grp > 0:
                            te.wait_ge(yt_ok, 2 * (grp - 1) + k + 1)
                        for b in range(4):
                            last = te.transpose(tp[k][:, b * P:(b + 1) * P], xn[q][:, b, k * P:(k + 1) * P], ident[:])
                        last.then_inc(tp_ok, 1)

                def prologue():
                    token_list(0, range(SL))
                    turn(0, 0)

                def step(e, t, p, lists_, ahead):
                    grp = e * NG + t
                    if t == 0:
                        te.wait_ge(w_in[p], 24 * (e - p) + 48)
                    te.wait_ge(yt_ok, 2 * grp + 2)
                    for m in range(FM):
                        if m >= 2:
                            te.wait_ge(gelu_ok, grp * FM + m - 1)
                        elif not (isinstance(e, int) and grp == 0):
                            te.wait_ge(gelu_ok, grp * FM + m - 1)
                        for k in range(2):
                            last = te.matmul(f1[m % 2][:], w1[p][:, k, m * P:(m + 1) * P], yt[t % 2][:, k, :],
                                             start=k == 0, stop=k == 1)
                        last.then_inc(f1_ok, 1)
                    if ahead >= 1:
                        turn(grp + 1, (t + 1) % 2)
                    te.wait_ge(gelu_ok, grp * FM + FM)
                    for b in range(4):
                        if not (isinstance(e, int) and grp == 0) and b % 2 == 0:
                            te.wait_ge(biased, 2 * (grp - 1) + b // 2 + 1)
                        for m in range(FM):
                            last = te.matmul(f2[b // 2][:, (b % 2) * 256:(b % 2 + 1) * 256],
                                             hb[t % 2][:, m, b * P:(b + 1) * P], w2[p][:, m, :],
                                             start=m == 0, stop=m == FM - 1)
                        last.then_inc(f2_ok, 1)
                    if lists_:
                        token_list(e + 1, range(4 * t, 4 * t + 4))

                run(te, prologue, step)

            @block.vector
            def _(dve):
                dve.wait_ge(iotas, 3)
                dve.wait_ge(small_in, 32)
                for dst, src in ((count, counti), (blk, blki), (pid, pidi)):
                    dve.tensor_copy(dst[:], src[:]).then_inc(consts, 1)
                dve.wait_ge(consts, 3)

                def list_rhs(e):
                    hi = d["hi"][:, :, bass.ds(e, 1), :].rearrange("p s a g -> p s (a g)")
                    if not (isinstance(e, int) and e == 0):
                        dve.wait_ge(oh_used, e * SL)
                        dve.wait_ge(rhs_ok, 3 * e)
                    dve.tensor_tensor(isin[:], hi.unsqueeze(3).to_broadcast([P, SL, G, 16]),
                                      count[:, 0:16].unsqueeze(1).unsqueeze(1).to_broadcast([P, SL, G, 16]),
                                      ALU.is_equal).then_inc(rhs_ok, 1)
                    dve.wait_ge(rhs_ok, 3 * e + 1)
                    dve.tensor_tensor(rhs[:, :, :, 0, :], isin[:], blk[:].unsqueeze(3).to_broadcast([P, SL, G, 16]),
                                      ALU.mult).then_inc(rhs_ok, 1)
                    dve.tensor_scalar(rhs[:, :, :, 1, :], isin[:], pid[:, 0:1], None, ALU.mult).then_inc(rhs_ok, 1)

                def list_onehot(e, s):
                    if not (isinstance(e, int) and e == 0 and s < 2):
                        dve.wait_ge(oh_used, e * SL + s - 1)
                    lo = d["lo"][:, s, bass.ds(e, 1), :].rearrange("p a g -> p (a g)")
                    dve.tensor_tensor(onehot[s % 2][:], lo.unsqueeze(2).to_broadcast([P, G, P]),
                                      count[:].unsqueeze(1).to_broadcast([P, G, P]), ALU.is_equal).then_inc(oh_ok, 1)

                def list_index(e, p):
                    dve.wait_ge(oh_used, (e + 1) * SL)
                    dve.tensor_copy(idxf[:], lists[:, 16:32]).then_inc(idxf_ok, 1)
                    dve.wait_ge(idxf_ok, e + 1)
                    if not isinstance(e, int) or e > 1:
                        for k in range(NG):
                            dve.wait_ge(added[k], 64 * (e - 1))
                    dve.scalar_tensor_tensor(idx[p][:], lists[:, 0:16], float(P), idxf[:], ALU.mult, ALU.add
                                             ).then_inc(idx_ok, 1)

                def normalise(grp, e, r, q):
                    dve.wait_ge(gathered[r], 64 * (e + 1))
                    if not isinstance(grp, int) or grp > 0:
                        dve.wait_ge(rstd_ok, grp)
                    for b in range(4):
                        last = dve.bn_stats(stats[:, b, :], xg[r][:, b, 0:256])
                    last.then_inc(st, 1)
                    dve.wait_ge(st, 2 * grp + 1)
                    dve.sem_inc(dve_passed, 1)
                    for b in range(4):
                        last = dve.bn_aggr(mv[:, b, :], stats[:, b, :])
                    last.then_inc(st, 1)
                    dve.wait_ge(st, 2 * grp + 2)
                    dve.tensor_scalar(ve[:], mv[:, :, 1], LN_EPS, None, ALU.add).then_inc(var_ok, 1)
                    if not isinstance(grp, int) or grp > 1:
                        dve.wait_ge(tp_ok, 2 * (grp - 1))
                    dve.wait_ge(rstd_ok, grp + 1)
                    for b in range(4):
                        last = dve.tensor_scalar(xn[q][:, b, :], xg[r][:, b, 0:256], mv[:, b, 0:1], rstd[:, b:b + 1],
                                                 ALU.subtract, ALU.mult)
                    last.then_inc(xn_ok, 1)

                def prologue():
                    list_rhs(0)
                    for s in range(SL):
                        list_onehot(0, s)
                    list_index(0, 0)
                    normalise(0, 0, 0, 0)

                def step(e, t, p, lists_, ahead):
                    grp = e * NG + t
                    if ahead >= 1:
                        normalise(grp + 1, e + (t + 1) // NG, (t + 1) % NG, (t + 1) % 2)
                    if lists_:
                        if t == 0:
                            list_rhs(e + 1)
                            for s in range(2):
                                list_onehot(e + 1, s)
                        else:
                            for s in range(4, 6):
                                list_onehot(e + 1, s)
                    if not isinstance(e, int) or grp > 1:
                        dve.wait_ge(added[(t - 2) % NG], 64 * (e + (1 if t >= 2 else 0)))
                    for i in range(2):
                        dve.wait_ge(f2_ok, grp * 4 + 2 * i + 2)
                        dve.tensor_tensor(ot[t % 2][:, 2 * i:2 * i + 2, :], f2[i][:].rearrange("p (b f) -> p b f", b=2),
                                          b2[:, bass.ds(e, 1), :].to_broadcast([P, 2, 256]), ALU.add).then_inc(biased, 1)
                    dve.wait_ge(biased, 2 * grp + 2)
                    for b in range(4):
                        s = xg[t][:, b, bass.ds(256 + e, 1)]
                        last = dve.tensor_scalar(ot[t % 2][:, b, :], ot[t % 2][:, b, :], s, None, ALU.mult)
                    last.then_inc(ot_ok, 1)
                    if lists_:
                        for s in range(4 * t + 2, 4 * t + 4):
                            list_onehot(e + 1, s)
                        if t == 1:
                            list_index(e + 1, 1 - p)

                run(dve, prologue, step)


def stage4(nc, d, n_tok):
    R, NBUF = 4, 4
    n = n_tok // (P * R)
    with ExitStack() as ctx:
        a = Alloc(nc, ctx)
        half = a.sb("half4", [P, R])
        x = [a.sb(f"rows{i}", [P, R, 256]) for i in range(NBUF)]
        stats = a.sb("stats4", [P, R, 6])
        mv = [a.sb(f"mv4_{i}", [P, R, 2]) for i in range(2)]
        ve = [a.sb(f"ve4_{i}", [P, R]) for i in range(2)]
        rstd = [a.sb(f"rstd4_{i}", [P, R]) for i in range(2)]
        passed = a.sem("passed4")
        half_ok = a.sem("half4_ready")
        x_in = [a.sem(f"rows_in{i}") for i in range(NBUF)]
        x_out = [a.sem(f"rows_out{i}") for i in range(NBUF)]
        st, var_ok, rstd_ok, normed = a.sem("stats4_steps"), a.sem("variance4"), a.sem("rstd4_ready"), a.sem("normed4")
        view = d["acc"].rearrange("(n p r) f -> n p r f", p=P, r=R)
        out = d["out"].rearrange("(n p r) f -> n p r f", p=P, r=R)
        with nc.Block() as block:

            @block.sync
            def _(sp):
                def load(i, b):
                    sp.dma_start(x[b][:], view[bass.ds(i, 1)].rearrange("a p r f -> p (a r) f")).then_inc(x_in[b], 16)

                for b in range(NBUF):
                    load(b, b)
                with sp.Fori(1, n // NBUF) as j:
                    for b in range(NBUF):
                        sp.wait_ge(x_out[b], 16 * j)
                        load(NBUF * j + b, b)

            @block.scalar
            def _(act):
                with act.Fori(0, n // NBUF) as j:
                    for b in range(NBUF):
                        i = NBUF * j + b
                        act.wait_ge(normed, i + 1)
                        act.dma_start(out[bass.ds(i, 1)].rearrange("a p r f -> p (a r) f"), x[b][:]).then_inc(x_out[b], 16)
                for b in range(NBUF):
                    act.wait_ge(x_out[b], 16 * n // NBUF)

            @block.gpsimd
            def _(pool):
                pool.memset(half[:], -0.5).then_inc(half_ok, 1)
                pool.wait_ge(half_ok, 1)
                with pool.Fori(0, n // 2) as j:
                    for b in range(2):
                        pool.wait_ge(var_ok, 2 * j + b + 1)
                        pool.tensor_tensor(rstd[b][:], ve[b][:], half[:], ALU.pow).then_inc(rstd_ok, 1)

            @block.vector
            def _(dve):
                def row_stats(i, j, b):
                    dve.wait_ge(x_in[b], 16 * (j + 1))
                    for r in range(R):
                        last = dve.bn_stats(stats[:, r, :], x[b][:, r, :])
                    last.then_inc(st, 1)
                    dve.wait_ge(st, 2 * i + 1)
                    dve.sem_inc(passed, 1)
                    for r in range(R):
                        last = dve.bn_aggr(mv[b % 2][:, r, :], stats[:, r, :])
                    last.then_inc(st, 1)
                    dve.wait_ge(st, 2 * i + 2)
                    dve.tensor_scalar(ve[b % 2][:], mv[b % 2][:, :, 1], LN_EPS, None, ALU.add).then_inc(var_ok, 1)

                def norm(i, b):
                    dve.wait_ge(rstd_ok, i + 1)
                    for r in range(R):
                        last = dve.tensor_scalar(x[b][:, r, :], x[b][:, r, :], mv[b % 2][:, r, 0:1],
                                                 rstd[b % 2][:, r:r + 1], ALU.subtract, ALU.mult)
                    last.then_inc(normed, 1)

                row_stats(0, 0, 0)
                with dve.Fori(0, n // NBUF - 1) as j:
                    for b in range(NBUF):
                        row_stats(NBUF * j + b + 1, j + (b + 1) // NBUF, (b + 1) % NBUF)
                        norm(NBUF * j + b, b)
                for b in range(NBUF):
                    if b + 1 < NBUF:
                        row_stats(n - NBUF + b + 1, n // NBUF - 1, b + 1)
                    norm(n - NBUF + b, b)


def program(nc, d, n_tok, n_batch):
    with ExitStack() as ctx:
        a = Alloc(nc, ctx)
        d["scores"] = a.sb("scores", [P, n_tok // P, 8])[:]
        stage1(nc, d, n_tok // CH, n_tok // n_batch // CH)
        d["lo"] = a.sb("lo", [P, n_tok // (16 * P), 8, 16], BF16)[:]
        d["hi"] = a.sb("hi", [P, n_tok // (16 * P), 8, 16], BF16)[:]
        stage2(nc, d, n_tok)
        stage3(nc, d, n_tok)
        stage4(nc, d, n_tok)


def kernel(**inputs):
    import numpy as np
    import concourse.bacc as bacc
    from concourse.bass_utils import run_bass_kernel_spmd

    c = np.ascontiguousarray
    at = {k[3:]: np.asarray(v) for k, v in inputs.items()}
    x = at["attn_hidden_states"]
    n_batch, seq, dm = x.shape
    n_tok = n_batch * seq
    xf = x.reshape(n_tok, dm)

    def tiles(w, n):
        return c(w.reshape((n, P) + w.shape[1:]).swapaxes(0, 1))

    vecs = np.stack([at["attn_conv1d_b"], at["attn_dt_proj_b"], at["attn_D_param"]])
    lnv = np.stack([at["ffn_ln_w"], at["ffn_ln_b"]])
    w1 = at["ffn_fc1s"].transpose(0, 2, 1)
    w2 = at["ffn_fc2s"].transpose(0, 2, 1)
    arrays = dict(
        x=c(xf), xt=c(xf.T), win=tiles(at["attn_in_proj_w"].T, 2), wconv=tiles(at["attn_conv1d_w"], 4),
        wx=tiles(at["attn_x_proj_w"].T, 4), wdt=c(at["attn_dt_proj_w"].T), wo=tiles(at["attn_out_proj_w"].T, 4),
        gate=tiles(at["ffn_gate_w"].T, 2), vecs=c(vecs.reshape(3, 4, P).transpose(2, 0, 1)),
        alog=tiles(at["attn_A_log"], 4),
        w1=c(w1.reshape(8, 2, P, 1024).transpose(0, 2, 1, 3)), w2=c(w2.reshape(8, 8, P, 256).transpose(0, 2, 1, 3)),
        b1=c(at["ffn_b1s"].reshape(8, 8, P).transpose(0, 2, 1)), b2=c(at["ffn_b2s"].reshape(8 * 256)),
        ln=c(lnv.reshape(2, 2, P).transpose(2, 0, 1)))
    nc = bacc.Bacc("TRN2", target_bir_lowering=False, num_devices=1)
    d = {k: nc.dram_tensor(f"in_{k}", v.shape, F32, kind="ExternalInput").ap() for k, v in arrays.items()}
    d["b_rows"] = nc.dram_tensor("b_rows", [2, 16, CH], F32).ap()
    d["x1s"] = nc.dram_tensor("x1_scores", [n_tok, 264], F32).ap()
    d["acc"] = nc.dram_tensor("sums", [n_tok, dm], F32).ap()
    d["out"] = nc.dram_tensor("out", [n_tok, dm], F32, kind="ExternalOutput").ap()
    program(nc, d, n_tok, n_batch)
    r = run_bass_kernel_spmd(nc, [{f"in_{k}": v for k, v in arrays.items()}], core_ids=[0])
    return r.results[0]["out"].reshape(n_batch, seq, dm)
```

```python
from contextlib import ExitStack

import concourse.bass as bass
from concourse import mybir

F32 = mybir.dt.float32
BF16 = mybir.dt.bfloat16
I32 = mybir.dt.int32
ALU = mybir.AluOpType
ACT = mybir.ActivationFunctionType
AX = mybir.AxisListType
P = 128
CH = 512
NB = CH // P
LN_EPS = 1e-5


class Alloc:

    def __init__(self, nc, ctx):
        self.nc, self.ctx = nc, ctx

    def sb(self, name, shape, dt=F32):
        return self.ctx.enter_context(self.nc.sbuf_tensor(name, shape, dt))

    def ps(self, name, shape, dt=F32):
        return self.ctx.enter_context(self.nc.psum_tensor(name, shape, dt))

    def sem(self, name):
        return self.ctx.enter_context(self.nc.semaphore(name))


STEPS = [(0, "X", 0), (0, "X", 1), (1, "X", 2), (1, "X", 3), (2, "Y", 0), (2, "C", 0),
         (3, "Y", 1), (3, "C", 1), (4, "Y", 2), (4, "C", 2), (5, "Y", 3), (5, "C", 3), (6, "T", 0), (6, "T", 1),
         (7, "XP", 0), (8, "CT", 0), (8, "D", 0), (9, "D", 1), (9, "D", 2), (10, "D", 3), (10, "L", 0),
         (11, "Z", 0), (11, "Z", 1), (12, "Z", 2), (12, "Z", 3), (13, "O", 0), (14, "O", 1)]
SPARE = 2
DA_RING, HT_RING = 4, 4
GROUP = {"X": "front", "C": "front", "XP": "front", "CT": "front", "D": "front", "Z": "front",
         "Y": "post1", "O": "post1", "T": "post2", "L": "post2"}
BANK = {(kind, i): n % SPARE for n, (_, kind, i) in enumerate(STEPS)}
ORDER = {g: [(k, i) for _, k, i in STEPS if GROUP[k] == g] for g in ("front", "post1", "post2")}
N_FRONT, N_POST1 = len(ORDER["front"]), len(ORDER["post1"])
LAG = {"front": -1, "post1": 1, "post2": 2}


DU = [("delta", 0), ("delta", 1), ("du", 0), ("delta", 2), ("du", 1), ("delta", 3), ("du", 2), ("du", 3)]
DU_AT = {14: (0, 1, 2, 3), 15: (4, 5, 6, 7)}
GATE_AT = 5
SILU_AT, SILU_Z_AT, SOFTPLUS_AT, DOUBLE_AT, ROUTER_EXP_AT = 7, 1, 12, 5, 13
NORM_AT, ROUTER_AT, ROUTER_END_AT, STATS_AT = 3, 11, 14, 15


def steps_of(groups):
    return [(slot, kind, i) for slot, kind, i in STEPS if GROUP[kind] in groups]


def last_use(m, ring):
    return next(k for k in range(1, 64) if (m - k) % 64 % ring == m % ring)


def nth(kind, i):
    return ORDER[GROUP[kind]].index((kind, i)) + 1


def stage1(nc, d, n_chunks, per_batch):
    DT, NS = 4, 16
    FR, P1, P2 = "front", "post1", "post2"
    BS = 4
    SM = 5
    assert per_batch % 4 == 0
    with ExitStack() as ctx:
        a = Alloc(nc, ctx)
        ident = a.sb("ident", [P, P])
        win = a.sb("win", [P, 2, 1024])
        wconv = a.sb("wconv", [P, DT, 4])
        conv = a.sb("conv", [P, DT, 4, P])
        wx = a.sb("wx", [P, DT, 48])
        wdt = a.sb("wdt", [16, 512])
        wo = a.sb("wo", [P, DT, 256])
        gate = a.sb("gate", [P, 2, 8])
        vecs = a.sb("vecs", [P, 3, DT])
        negA = a.sb("negA", [P, DT, NS])
        half = a.sb("half", [P, NB])
        keep_h = a.sb("keep_h", [P, 1], I32)
        keep_x = a.sb("keep_x", [P, 1], I32)
        xin = a.sb("xin", [P, 2, CH])
        xh = a.sb("xh", [P, DT, 3 + CH])
        u = [a.sb(f"u{i}", [P, DT, CH]) for i in range(2)]
        dl = [a.sb(f"dl{i}", [P, DT, CH]) for i in range(2)]
        du = [a.sb(f"du{i}", [P, DT, CH]) for i in range(2)]
        sz = [a.sb(f"sz{i}", [P, DT, CH]) for i in range(2)]
        xdbl = a.sb("xdbl", [48, CH])
        ct = [a.sb(f"ct{i}", [P, NB, NS]) for i in range(2)]
        bb = [a.sb(f"bb{i}", [P, BS, CH]) for i in range(2)]
        dbu = [a.sb(f"dbu{i}", [P, DT, CH]) for i in range(2)]
        h = [a.sb(f"h{i}", [P, DT, CH]) for i in range(2)]
        hlast = a.sb("hlast", [P, NS, DT])
        carry = a.sb("carry", [P, NS, DT])
        acc = [a.sb(f"acc{i}", [P, NB, 512]) for i in range(2)]
        g = a.sb("g", [P, DT, CH])
        xres = a.sb("xres", [P, NB, 256])
        stats = a.sb("stats", [P, NB, 6])
        mv = a.sb("mv", [P, NB, 2])
        ve = a.sb("ve", [P, NB])
        rstd = a.sb("rstd", [P, NB])
        shift = a.sb("shift", [P, NB])
        x2 = a.sb("x2", [P, NB, 256])
        x1t = x2[:].rearrange("p (i b) f -> p i (b f)", i=2)
        lg = a.sb("lg", [P, NB, 8])
        mx = a.sb("mx", [P, NB])
        ssum = a.sb("ssum", [P, NB])
        da = [(a.ps if i < 2 else a.sb)(f"da{i}", [P, CH]) for i in range(DA_RING)]
        ht = [a.ps(f"ht{i}", [P, 512]) for i in range(HT_RING)]
        spare = [a.ps(f"spare{i}", [P, 512]) for i in range(SPARE)]

        S = a.sem
        te_passed, dve_passed, sp_passed = S("te_passed"), S("dve_passed"), S("sp_passed")
        loaded, ident_ok = S("weights_loaded"), S("ident_ready")
        set_ok, negA_ok, conv_ok = S("constants_set"), S("negA_ready"), S("conv_ready")
        exp_done, dbu_done, scan_done, tr_done, mac_done = (
            S("exp_done"), S("dbu_done"), S("scan_done"), S("turned"), S("mac_done"))
        last_saved, carry_ok, halo_ok = S("last_saved"), S("carry_ready"), S("halo_ready")
        keep_h_ok, keep_x_ok = S("keep_h_toggled"), S("keep_x_toggled")
        pe = {FR: S("pe_front"), P1: S("pe_post1"), P2: S("pe_post2")}
        out_of = {FR: S("front_evacuated"), P1: S("post1_evacuated"), P2: S("post2_evacuated")}
        silu_u, silu_z, soft = S("silu_u"), S("silu_z"), S("softplus_steps")
        du_ok, gated, var_ok, rstd_ok = S("du_steps"), S("gated"), S("variance_ready"), S("rstd_ready")
        stats_ok, normed, doubled = S("stats_steps"), S("x1_ready"), S("x1_doubled")
        shift_ok = S("shift_ready")
        exp_l, sm = S("router_exp"), S("router_steps")
        xin_in, xres_in, b_out, b_in = (
            S("xin_in"), S("xres_in"), S("b_out"), [S(f"b_in{i}") for i in range(2)])
        x1_out, x2_out = S("x1_out"), S("x2_out")

        def step_done(kind, i, c):
            grp = GROUP[kind]
            k = c - LAG[grp]
            if kind == "L":
                return sm, k * SM + 2
            per = {FR: N_FRONT, P1: N_POST1, P2: 2}[grp]
            return out_of[grp], k * per + nth(kind, i)

        def pe_done(kind, i, c):
            grp = GROUP[kind]
            return pe[grp], (c - LAG[grp]) * len(ORDER[grp]) + nth(kind, i)

        with nc.Block() as block:

            @block.sync
            def _(sp):
                for dst, src in ((win, d["win"]), (wconv, d["wconv"]), (wx, d["wx"]), (wdt, d["wdt"]),
                                 (wo, d["wo"]), (gate, d["gate"]), (vecs, d["vecs"]), (negA, d["alog"])):
                    sp.dma_start(dst[:], src).then_inc(loaded, 16)

                def load_xin(f):
                    sp.dma_start(xin[:], d["xt"][:, bass.ds(f * CH, CH)].rearrange("(k p) t -> p k t", p=P)
                                 ).then_inc(xin_in, 16)

                def b_write(f, q):
                    s, v = step_done("XP", 0, f - 1)
                    sp.wait_ge(s, v)
                    sp.dma_start(d["b_rows"][q], xdbl[16:32, :]).then_inc(b_out, 16)

                def b_read(f, q, part):
                    if part == 0:
                        sp.wait_ge(b_out, 16 * f + 16)
                        sp.sem_inc(sp_passed, 1)
                    if not (isinstance(f, int) and f == 0 and part < 2):
                        sp.wait_ge(dbu_done, f * NS + (part - 1) * BS)
                    sp.dma_start(bb[part % 2][:], d["b_rows"][q, BS * part:BS * part + BS, :].partition_broadcast(P)
                                 ).then_inc(b_in[part % 2], 16)

                def chunk(c, q, groups, more, scan=True):
                    if scan:
                        b_read(c, q, 2)
                    if P2 in groups:
                        sp.wait_ge(normed, c - 1)
                        sp.dma_start(rows(d["x1s"], c - 2)[:, :, 0:256], xres[:]).then_inc(x1_out, 16)
                        sp.wait_ge(doubled, c - 1)
                        sp.dma_start(rows(d["acc"], c - 2), x2[:]).then_inc(x2_out, 16)
                    if P1 in groups:
                        if P2 in groups:
                            s, v = pe_done("T", 1, c)
                            sp.wait_ge(s, v)
                            sp.sem_inc(sp_passed, 1)
                            sp.wait_ge(x1_out, 16 * (c - 1))
                        sp.dma_start(xres[:], rows(d["x"], c - 1)).then_inc(xres_in, 16)
                    if scan:
                        b_read(c, q, 3)
                    if FR in groups:
                        b_write(c + 1, 1 - q)
                        b_read(c + 1, 1 - q, 0)
                        if more:
                            s, v = pe_done("Z", 3, c)
                            sp.wait_ge(s, v)
                            load_xin(c + 2)
                        b_read(c + 1, 1 - q, 1)

                def rows(t, c):
                    return t[bass.ds(c * CH, CH), :].rearrange("(b p) f -> p b f", p=P)

                load_xin(0)
                b_write(0, 0)
                b_read(0, 0, 0)
                b_read(0, 0, 1)
                s, v = pe_done("Z", 3, -1)
                sp.wait_ge(s, v)
                load_xin(1)
                chunk(0, 0, (FR,), True)
                chunk(1, 1, (FR, P1), True)
                with sp.Fori(1, n_chunks // 2 - 1) as j:
                    chunk(2 * j, 0, (FR, P1, P2), True)
                    chunk(2 * j + 1, 1, (FR, P1, P2), True)
                chunk(n_chunks - 2, 0, (FR, P1, P2), False)
                chunk(n_chunks - 1, 1, (P1, P2), False)
                chunk(n_chunks, 0, (P1, P2), False, False)
                chunk(n_chunks + 1, 1, (P2,), False, False)
                sp.wait_ge(x1_out, 16 * n_chunks)
                sp.wait_ge(x2_out, 16 * n_chunks)

            @block.gpsimd
            def _(pool):
                pool.memset(ident[:], 0.0).then_inc(ident_ok, 1)
                pool.memset(half[:], -0.5).then_inc(set_ok, 1)
                pool.memset(keep_h[:], -1).then_inc(keep_h_ok, 1)
                pool.memset(keep_x[:], -1).then_inc(keep_x_ok, 1)
                pool.wait_ge(ident_ok, 1)
                pool.affine_select(out=ident[:], in_=ident[:], compare_op=ALU.not_equal, fill=1.0, base=0,
                                   pattern=[[-1, P]], channel_multiplier=1).then_inc(ident_ok, 1)

                def delta_u(f, q, pieces):
                    for k in pieces:
                        what, dt = DU[k]
                        if k == 0:
                            pool.wait_ge(soft, 2 * f + 2)
                        if what == "delta":
                            pool.tensor_tensor(dl[q][:, dt, :], dl[q][:, dt, :], du[q][:, dt, :],
                                               ALU.add).then_inc(du_ok, 1)
                        else:
                            pool.wait_ge(du_ok, f * len(DU) + DU.index(("delta", dt)) + 1)
                            pool.tensor_tensor(du[q][:, dt, :], dl[q][:, dt, :], u[q][:, dt, :],
                                               ALU.mult).then_inc(du_ok, 1)

                def gating(c, q, i):
                    s, v = step_done("Y", i, c)
                    pool.wait_ge(s, v)
                    if i == 0:
                        pool.wait_ge(silu_z, c)
                    pool.tensor_tensor(g[:, i, :], g[:, i, :], sz[q][:, i, :], ALU.mult).then_inc(gated, 1)

                def chunk(c, q, groups, scan=True):
                    for n in range(NS if scan else 1):
                        if scan:
                            if n == 0:
                                pool.wait_ge(du_ok, (c + 1) * len(DU))
                            part, m = divmod(n, BS)
                            if m == 0:
                                pool.wait_ge(b_in[part % 2], 16 * (c * (NS // BS // 2) + part // 2) + 16)
                            if not (isinstance(c, int) and c == 0 and n < 2):
                                pool.wait_ge(scan_done, (c * NS + n - 1) * DT)
                            pool.tensor_tensor(dbu[n % 2][:], du[q][:],
                                               bb[part % 2][:, m:m + 1, :].to_broadcast([P, DT, CH]),
                                               ALU.mult).then_inc(dbu_done, 1)
                        if P2 in groups and n == (1 if scan else 0):
                            pool.wait_ge(var_ok, c - 1)
                            pool.tensor_tensor(rstd[:], ve[:], half[:], ALU.pow).then_inc(rstd_ok, 1)
                        if P1 in groups:
                            for i in range(DT):
                                if n == GATE_AT + i or not scan:
                                    gating(c, 1 - q, i)
                        if FR in groups and n in DU_AT:
                            delta_u(c + 1, 1 - q, DU_AT[n])

                chunk(0, 0, (FR,))
                chunk(1, 1, (FR, P1))
                with pool.Fori(1, n_chunks // 2 - 1) as j:
                    chunk(2 * j, 0, (FR, P1, P2))
                    chunk(2 * j + 1, 1, (FR, P1, P2))
                chunk(n_chunks - 2, 0, (FR, P1, P2))
                chunk(n_chunks - 1, 1, (P1, P2))
                chunk(n_chunks, 0, (P1, P2), False)
                chunk(n_chunks + 1, 1, (P2,), False)

            @block.scalar
            def _(act):
                act.wait_ge(loaded, 16 * 8)
                act.activation(negA[:], negA[:], ACT.Exp).then_inc(negA_ok, 1)
                act.wait_ge(negA_ok, 1)
                act.mul(negA[:], negA[:], -1.0).then_inc(negA_ok, 1)
                act.wait_ge(negA_ok, 2)

                def exps(c, q, n):
                    for dt in range(DT):
                        e = (c * NS + n) * DT + dt
                        if n == 0:
                            act.wait_ge(du_ok, c * len(DU) + DU.index(("delta", dt)) + 1)
                        m = n * DT + dt
                        if not (isinstance(c, int) and c == 0 and m < DA_RING):
                            act.wait_ge(scan_done, e - last_use(m, DA_RING) + 1)
                        act.activation(da[m % DA_RING][:], dl[q][:, dt, :], ACT.Exp,
                                       scale=negA[:, dt, n:n + 1]).then_inc(exp_done, 1)

                def save_last(c, n):
                    act.wait_ge(scan_done, (c * NS + n + 1) * DT)
                    act.copy(hlast[:, n, :], h[n % 2][:, :, CH - 1]).then_inc(last_saved, 1)

                def evacuate(kind, i, c, q):
                    bank = spare[BANK[kind, i]]
                    s, v = pe_done(kind, i, c)
                    act.wait_ge(s, v)
                    done = out_of[GROUP[kind]]
                    f = c + 1
                    if kind == "X":
                        if i == 0:
                            act.wait_ge(halo_ok, f + 1)
                        act.copy(xh[:, i, 3:], bank[:]).then_inc(done, 1)
                    elif kind == "C":
                        if not (isinstance(c, int) and c < 1):
                            s, v = step_done("Y", i, c)
                            act.wait_ge(s, v)
                        act.activation(u[q][:, i, :], bank[:], ACT.Identity,
                                       bias=vecs[:, 0, i:i + 1]).then_inc(done, 1)
                    elif kind == "Z":
                        if i == 0 and not (isinstance(c, int) and c < 1):
                            act.wait_ge(gated, DT * c)
                        act.copy(sz[q][:, i, :], bank[:]).then_inc(done, 1)
                    elif kind == "XP":
                        if not (isinstance(f, int) and f == 0):
                            act.wait_ge(b_out, 16 * f)
                        act.copy(xdbl[:], bank[0:48, :]).then_inc(done, 1)
                    elif kind == "CT":
                        act.copy(ct[q][:], bank[:, 0:NB * 48].rearrange("p (b r) -> p b r", b=NB)[:, :, 32:48]
                                 ).then_inc(done, 1)
                    elif kind == "D":
                        if not (isinstance(f, int) and f < 2):
                            act.wait_ge(dbu_done, (f - 1) * NS)
                        act.activation(dl[q][:, i, :], bank[:], ACT.Abs, bias=vecs[:, 1, i:i + 1])
                        act.activation(du[q][:, i, :], bank[:], ACT.Relu,
                                       bias=vecs[:, 1, i:i + 1]).then_inc(done, 1)
                    elif kind == "T":
                        if i == 0:
                            act.wait_ge(x2_out, 16 * (c - 1))
                        act.copy(x1t[:, i, :], bank[:]).then_inc(done, 1)

                def silu_of_u(f, q):
                    s, v = step_done("C", 3, f - 1)
                    act.wait_ge(s, v)
                    act.activation(u[q][:], u[q][:], ACT.Silu).then_inc(silu_u, 1)

                def silu_of_z(c, q):
                    s, v = step_done("Z", 3, c - 1)
                    act.wait_ge(s, v)
                    act.activation(sz[q][:], sz[q][:], ACT.Silu).then_inc(silu_z, 1)

                def softplus(f, q):
                    s, v = step_done("D", 3, f - 1)
                    act.wait_ge(s, v)
                    act.activation(dl[q][:], dl[q][:], ACT.Exp, scale=-1.0).then_inc(soft, 1)
                    act.wait_ge(soft, 2 * f + 1)
                    act.activation(dl[q][:], dl[q][:], ACT.Ln, bias=1.0).then_inc(soft, 1)

                def chunk(c, q, groups, scan=True):
                    todo = steps_of(groups)
                    for n in range(NS + 2):
                        if scan and n < NS:
                            exps(c, q, n)
                            if n > 0:
                                save_last(c, n - 1)
                        if n == 0 and not (isinstance(c, int) and c == 0) and (scan or P1 in groups and P2 in groups):
                            save_last(c - 1, NS - 1)
                        for slot, kind, i in todo:
                            if slot == n - 2 and kind not in ("Y", "O", "L"):
                                evacuate(kind, i, c, 1 - q)
                        if n == SILU_AT:
                            if FR in groups:
                                silu_of_u(c + 1, 1 - q)
                        if n == SILU_Z_AT and scan:
                            silu_of_z(c, q)
                        if n == SOFTPLUS_AT and FR in groups:
                            softplus(c + 1, 1 - q)
                        if n == NORM_AT + 1 and P2 in groups:
                            act.wait_ge(shift_ok, c - 1)
                            for b in range(NB):
                                last = act.activation(xres[:, b, :], xres[:, b, :], ACT.Identity,
                                                      bias=shift[:, b:b + 1], scale=rstd[:, b:b + 1])
                            last.then_inc(normed, 1)
                        if n == DOUBLE_AT and P2 in groups:
                            act.wait_ge(normed, c - 1)
                            act.mul(x2[:], xres[:], 2.0).then_inc(doubled, 1)
                        if n == ROUTER_EXP_AT and P2 in groups:
                            act.wait_ge(sm, (c - 2) * SM + 2)
                            act.activation(lg[:], lg[:], ACT.Exp).then_inc(exp_l, 1)

                for _, kind, i in steps_of((FR,)):
                    if (kind, i) == ("XP", 0):
                        silu_of_u(0, 0)
                    evacuate(kind, i, -1, 0)
                    if (kind, i) == ("D", 3):
                        softplus(0, 0)
                chunk(0, 0, (FR,))
                chunk(1, 1, (FR, P1))
                with act.Fori(1, n_chunks // 2 - 1) as j:
                    chunk(2 * j, 0, (FR, P1, P2))
                    chunk(2 * j + 1, 1, (FR, P1, P2))
                chunk(n_chunks - 2, 0, (FR, P1, P2))
                chunk(n_chunks - 1, 1, (P1, P2))
                chunk(n_chunks, 0, (P1, P2), False)
                chunk(n_chunks + 1, 1, (P2,), False)

            @block.tensor
            def _(te):
                te.wait_ge(loaded, 16 * 8)
                te.wait_ge(ident_ok, 2)
                te.wait_ge(conv_ok, 1)

                def step(kind, i, c, q, prev):
                    bank = spare[BANK[kind, i]]
                    if prev:
                        s, v = step_done(*prev)
                        te.wait_ge(s, v)
                    f, p = c + 1, c - 1
                    done = pe[GROUP[kind]]
                    if kind in ("X", "Z"):
                        if kind == "X" and i == 0:
                            te.wait_ge(xin_in, 16 * f + 16)
                        col = (512 if kind == "Z" else 0) + i * P
                        for k in range(2):
                            last = te.matmul(bank[:], win[:, k, col:col + P], xin[:, k, :],
                                             start=k == 0, stop=k == 1)
                    elif kind == "C":
                        s, v = step_done("X", i, c)
                        te.wait_ge(s, v)
                        for k in range(4):
                            last = te.matmul(bank[:], conv[:, i, k, :], xh[:, i, k:k + CH],
                                             start=k == 0, stop=k == 3)
                    elif kind == "XP":
                        te.wait_ge(silu_u, f + 1)
                        for k in range(DT):
                            last = te.matmul(bank[0:48, :], wx[:, k, :], u[q][:, k, :],
                                             start=k == 0, stop=k == DT - 1)
                    elif kind == "CT":
                        s, v = step_done("XP", 0, c)
                        te.wait_ge(s, v)
                        te.sem_inc(te_passed, 1)
                        for b in range(NB):
                            last = te.transpose(bank[:, b * 48:b * 48 + 48], xdbl[:, b * P:(b + 1) * P],
                                                ident[0:48, 0:48])
                    elif kind == "D":
                        last = te.matmul(bank[:], wdt[:, i * P:(i + 1) * P], xdbl[0:16, :],
                                         start=True, stop=True)
                    elif kind == "Y":
                        if i == 0:
                            te.wait_ge(mac_done, c * NS * NB)
                        for b in range(NB):
                            last = te.transpose(bank[:, b * P:(b + 1) * P], acc[q][:, b, i * P:(i + 1) * P],
                                                ident[:])
                    elif kind == "O":
                        if i == 0:
                            te.wait_ge(gated, DT * (p + 1))
                        for b in range(2):
                            for k in range(DT):
                                t0 = (2 * i + b) * P
                                last = te.matmul(bank[:, b * 256:(b + 1) * 256], g[:, k, t0:t0 + P], wo[:, k, :],
                                                 start=k == 0, stop=k == DT - 1)
                    elif kind == "T":
                        if i == 0:
                            te.wait_ge(normed, c - 1)
                        for b in range(2):
                            for k in range(2):
                                last = te.transpose(bank[:, (2 * b + k) * P:(2 * b + k + 1) * P],
                                                    xres[:, 2 * i + b, k * P:(k + 1) * P], ident[:])
                    elif kind == "L":
                        s, v = step_done("T", 1, c)
                        te.wait_ge(s, v)
                        for b in range(NB):
                            for k in range(2):
                                o = (2 * (b % 2) + k) * P
                                last = te.matmul(bank[:, b * 8:b * 8 + 8], x1t[:, b // 2, o:o + P], gate[:, k, :],
                                                 start=k == 0, stop=k == 1)
                    last.then_inc(done, 1)

                def turn(c, n, blocks):
                    for b in blocks:
                        m = n * NB + b
                        if b == 0:
                            te.wait_ge(scan_done, c * NS * DT + n * DT + DT)
                        if not (isinstance(c, int) and c == 0 and m < HT_RING):
                            te.wait_ge(mac_done, c * NS * NB + m - last_use(m, HT_RING) + 1)
                        for dt in range(DT):
                            last = te.transpose(ht[m % HT_RING][:, dt * P:(dt + 1) * P],
                                                h[n % 2][:, dt, b * P:(b + 1) * P], ident[:])
                        last.then_inc(tr_done, 1)

                def chunk(c, q, groups, before, scan=True):
                    todo, used = steps_of(groups), steps_of(before)
                    for n in range(NS):
                        if scan:
                            turn(c, n, range(HT_RING))
                        for k, (slot, kind, i) in enumerate(todo):
                            if slot != n:
                                continue
                            same = [(x, y, c) for _, x, y in todo[:k] if BANK[x, y] == BANK[kind, i]]
                            wrap = [(x, y, c - 1) for _, x, y in used if BANK[x, y] == BANK[kind, i]]
                            prev = (same or wrap or [None])[-1]
                            step(kind, i, c, 1 - q, prev)
                        if scan:
                            turn(c, n, range(HT_RING, NB))

                prev_of = {}
                for _, kind, i in steps_of((FR,)):
                    step(kind, i, -1, 0, prev_of.get(BANK[kind, i]))
                    prev_of[BANK[kind, i]] = (kind, i, -1)
                chunk(0, 0, (FR,), (FR,))
                chunk(1, 1, (FR, P1), (FR,))
                with te.Fori(1, n_chunks // 2 - 1) as j:
                    chunk(2 * j, 0, (FR, P1, P2), (FR, P1, P2))
                    chunk(2 * j + 1, 1, (FR, P1, P2), (FR, P1, P2))
                chunk(n_chunks - 2, 0, (FR, P1, P2), (FR, P1, P2))
                chunk(n_chunks - 1, 1, (P1, P2), (FR, P1, P2))
                chunk(n_chunks, 0, (P1, P2), (P1, P2), False)
                chunk(n_chunks + 1, 1, (P2,), (P1, P2), False)

            @block.vector
            def _(dve):
                dve.wait_ge(loaded, 16 * 8)
                dve.wait_ge(ident_ok, 2)
                for dt in range(DT):
                    for k in range(4):
                        last = dve.tensor_scalar(conv[:, dt, k, :], ident[:], wconv[:, dt, k:k + 1], None, ALU.mult)
                last.then_inc(conv_ok, 1)
                dve.memset(xh[:, :, 0:3], 0.0).then_inc(halo_ok, 1)

                dve.wait_ge(soft, 2)
                for what, dt in DU:
                    if what == "delta":
                        dve.tensor_tensor(dl[0][:, dt, :], dl[0][:, dt, :], du[0][:, dt, :], ALU.add).then_inc(du_ok, 1)
                    else:
                        dve.wait_ge(du_ok, DU.index(("delta", dt)) + 1)
                        dve.tensor_tensor(du[0][:, dt, :], dl[0][:, dt, :], u[0][:, dt, :], ALU.mult).then_inc(du_ok, 1)

                def scans(c, q, n):
                    unit = c * NS + n
                    first = isinstance(c, int) and c == 0
                    dve.wait_ge(dbu_done, unit + 1)
                    if not (first and n < 2):
                        dve.wait_ge(tr_done, (unit - 1) * NB)
                        dve.wait_ge(last_saved, unit - 1)
                    for dt in range(DT):
                        dve.wait_ge(exp_done, unit * DT + dt + 1)
                        start = 0.0 if first else (carry if q == 0 else hlast)[:, n, dt:dt + 1]
                        dve.tensor_tensor_scan(h[n % 2][:, dt, :], da[(n * DT + dt) % DA_RING][:],
                                              dbu[n % 2][:, dt, :], start, ALU.mult, ALU.add).then_inc(scan_done, 1)

                def macs(c, q, n):
                    unit = c * NS + n
                    for b in range(NB):
                        dve.wait_ge(tr_done, unit * NB + b + 1)
                        cc = ct[q][:, b, n:n + 1]
                        if n == 0:
                            if b == 0:
                                s, v = step_done("CT", 0, c - 1)
                                dve.wait_ge(s, v)
                                if not (isinstance(c, int) and c < 2):
                                    dve.wait_ge(pe[P1], (c - 2) * N_POST1 + nth("Y", 3))
                            ins = dve.tensor_scalar(acc[q][:, b, :], ht[(n * NB + b) % HT_RING][:], cc, None, ALU.mult)
                        else:
                            dve.wait_ge(mac_done, (unit - 1) * NB + b + 1)
                            ins = dve.scalar_tensor_tensor(acc[q][:, b, :], ht[(n * NB + b) % HT_RING][:], cc, acc[q][:, b, :],
                                                          ALU.mult, ALU.add)
                        ins.then_inc(mac_done, 1)

                def post1_step(kind, i, c, q):
                    p = c - 1
                    bank = spare[BANK[kind, i]]
                    s, v = pe_done(kind, i, c)
                    dve.wait_ge(s, v)
                    if kind == "Y":
                        if i == 0 and not (isinstance(c, int) and c == 1):
                            dve.wait_ge(pe[P1], (p - 1) * N_POST1 + nth("O", 1))
                        dve.scalar_tensor_tensor(g[:, i, :], u[q][:, i, :], vecs[:, 2, i:i + 1], bank[:],
                                                ALU.mult, ALU.add).then_inc(out_of[P1], 1)
                    else:
                        if i == 0:
                            dve.wait_ge(xres_in, 16 * c)
                        x = xres[:, 2 * i:2 * i + 2, :].rearrange("p b f -> p (b f)")
                        dve.tensor_tensor(x, bank[:], x, ALU.add).then_inc(out_of[P1], 1)

                def layer_stats(c):
                    p = c - 1
                    s, v = step_done("O", 1, c)
                    dve.wait_ge(s, v)
                    if not (isinstance(c, int) and c == 1):
                        dve.wait_ge(rstd_ok, p)
                    for b in range(NB):
                        last = dve.bn_stats(stats[:, b, :], xres[:, b, :])
                    last.then_inc(stats_ok, 1)
                    dve.wait_ge(stats_ok, 2 * p + 1)
                    dve.sem_inc(dve_passed, 1)
                    for b in range(NB):
                        last = dve.bn_aggr(mv[:, b, :], stats[:, b, :])
                    last.then_inc(stats_ok, 1)
                    dve.wait_ge(stats_ok, 2 * p + 2)
                    dve.tensor_scalar(ve[:], mv[:, :, 1], LN_EPS, None, ALU.add).then_inc(var_ok, 1)

                def layer_shift(c):
                    r = c - 2
                    dve.wait_ge(rstd_ok, r + 1)
                    dve.scalar_tensor_tensor(shift[:], mv[:, :, 0], -1.0, rstd[:], ALU.mult, ALU.mult
                                             ).then_inc(shift_ok, 1)

                def router(c, part):
                    r = c - 2
                    if part == 0:
                        s, v = pe_done("L", 0, c)
                        dve.wait_ge(s, v)
                        bank = spare[BANK["L", 0]][:, 0:NB * 8].rearrange("p (b e) -> p b e", b=NB)
                        dve.reduce_max(mx[:], bank, AX.X).then_inc(sm, 1)
                        dve.wait_ge(sm, r * SM + 1)
                        ins = dve.tensor_tensor(lg[:], bank, mx[:].unsqueeze(2).to_broadcast([P, NB, 8]), ALU.subtract)
                        ins.then_inc(sm, 1)
                    else:
                        dve.wait_ge(exp_l, r + 1)
                        dve.reduce_sum(ssum[:], lg[:], AX.X).then_inc(sm, 1)
                        dve.wait_ge(sm, r * SM + 3)
                        dve.reciprocal(ssum[:], ssum[:]).then_inc(sm, 1)
                        dve.wait_ge(sm, r * SM + 4)
                        dve.tensor_tensor(d["scores"][:, bass.ds(r * NB, NB), :], lg[:],
                                         ssum[:].unsqueeze(2).to_broadcast([P, NB, 8]), ALU.mult).then_inc(sm, 1)

                def chunk(c, q, groups, j, scan=True):
                    first = isinstance(c, int) and c == 0
                    todo = [(s, k, i) for s, k, i in steps_of(groups) if k in ("Y", "O")]
                    if scan and q == 0 and not first:
                        dve.wait_ge(last_saved, c * NS)
                        dve.wait_ge(keep_h_ok, j)
                        dve.tensor_scalar(carry[:].rearrange("p n d -> p (n d)").bitcast(I32),
                                         hlast[:].rearrange("p n d -> p (n d)").bitcast(I32),
                                         keep_h[:, 0:1], None, ALU.bitwise_and).then_inc(carry_ok, 1)
                        dve.wait_ge(carry_ok, j)
                        dve.tensor_scalar(keep_h[:], keep_h[:], -1, None, ALU.bitwise_xor).then_inc(keep_h_ok, 1)
                    for n in range(NS):
                        at = n - 1 if scan else n
                        summed = None
                        if scan and n > 0:
                            summed = (c, q, n - 1)
                        elif n == 0 and not first and (scan or P1 in groups and P2 in groups):
                            summed = (c - 1, 1 - q, NS - 1)
                        if scan:
                            scans(c, q, n)
                            if n == 0 and FR in groups:
                                halo(c + 1, 1 - q, j)
                        if summed:
                            macs(*summed)
                        for slot, kind, i in todo:
                            if slot == at and kind == "Y":
                                post1_step(kind, i, c, 1 - q)
                        for slot, kind, i in todo:
                            if slot == at and kind == "O":
                                post1_step(kind, i, c, 1 - q)
                        if P2 in groups and n == NORM_AT:
                            layer_shift(c)
                        if P2 in groups and n == ROUTER_AT:
                            router(c, 0)
                        if P2 in groups and n == ROUTER_END_AT:
                            router(c, 1)
                        if P1 in groups and n == STATS_AT:
                            layer_stats(c)

                def halo(f, q, j):
                    s, v = pe_done("C", 3, f - 2)
                    dve.wait_ge(s, v)
                    dst, src = xh[:, :, 0:3], xh[:, :, CH:CH + 3]
                    if q == 1:
                        dve.tensor_copy(dst, src).then_inc(halo_ok, 1)
                    else:
                        dve.wait_ge(keep_x_ok, j + 1)
                        dve.tensor_scalar(dst.bitcast(I32), src.bitcast(I32), keep_x[:, 0:1], None,
                                         ALU.bitwise_and).then_inc(halo_ok, 1)
                        dve.wait_ge(halo_ok, f + 1)
                        dve.tensor_scalar(keep_x[:], keep_x[:], -1, None, ALU.bitwise_xor).then_inc(keep_x_ok, 1)

                chunk(0, 0, (FR,), 0)
                chunk(1, 1, (FR, P1), 0)
                with dve.Fori(1, n_chunks // 2 - 1) as j:
                    chunk(2 * j, 0, (FR, P1, P2), j)
                    chunk(2 * j + 1, 1, (FR, P1, P2), j)
                last_pair = n_chunks // 2 - 1
                chunk(n_chunks - 2, 0, (FR, P1, P2), last_pair)
                chunk(n_chunks - 1, 1, (P1, P2), last_pair)
                chunk(n_chunks, 0, (P1, P2), last_pair + 1, False)
                chunk(n_chunks + 1, 1, (P2,), last_pair + 1, False)


def stage2(nc, d, n_tok):
    E, G = 8, 16
    SL = n_tok // (G * P)
    J = SL * P
    K = n_tok // E
    BITS = 30
    with ExitStack() as ctx:
        a = Alloc(nc, ctx)
        ident = a.sb("ident2", [P, P])
        same = a.sb("same_expert", [P, P])
        before = a.sb("groups_before", [P, P])
        ones = a.sb("ones", [P, J])
        sc = a.sb("sc", [P, J])
        gt = a.sb("gt", [P, J])
        eq = a.sb("eq", [P, J])
        run = a.sb("run", [P, J])
        pos = a.sb("pos", [P, J])
        slot = a.sb("slot", [P, J], I32)
        part = a.sb("part", [P, J], I32)
        thr = a.sb("thr", [P, 1], I32)
        bit = a.sb("bit", [P, 1], I32)
        cand = a.sb("cand", [P, 1], I32)
        take = a.sb("take", [P, 1], I32)
        cnt = a.sb("cnt", [P, 1])
        lim = a.sb("lim", [P, 1])
        off = a.sb("off", [P, 1])
        big = [a.ps(f"big{i}", [P, 512]) for i in range(2)]
        tot = a.ps("tot", [P, 4])
        made, const_ok, mats = a.sem("masks_made"), a.sem("constants2"), a.sem("masks_ready")
        counted_take = a.sem("count_compared")
        turned, sc_ok, counted, summed, step = (
            a.sem("scores_turned"), a.sem("scores_ready"), a.sem("counted"), a.sem("summed"), a.sem("bisect_step"))
        chain, sums, back = a.sem("select_step"), a.sem("select_sums"), a.sem("slots_turned")
        passed = a.sem("passed2")
        packed_ok = a.sem("scores_packed")
        packed = a.sb("packed", [P, SL, E * G])
        stored = a.sem("scores_stored")
        view = d["scores"].rearrange("p (g s) e -> p s e g", s=SL)
        with nc.Block() as block:

            @block.sync
            def _(sp):
                sp.dma_start(d["x1s"][:, 256:264].rearrange("(b p) e -> p b e", p=P), d["scores"]).then_inc(stored, 16)
                sp.wait_ge(stored, 16)

            @block.gpsimd
            def _(pool):
                for m, v in ((ident, 0.0), (same, 1.0)):
                    pool.memset(m[:], v).then_inc(made, 1)
                pool.memset(ones[:], 1.0).then_inc(const_ok, 1)
                pool.memset(thr[:], 0).then_inc(const_ok, 1)
                pool.memset(bit[:], 1 << (BITS - 1)).then_inc(step, 1)
                pool.wait_ge(made, 2)
                pool.affine_select(out=ident[:], in_=ident[:], compare_op=ALU.not_equal, fill=1.0, base=0,
                                   pattern=[[-1, P]], channel_multiplier=1).then_inc(mats, 1)
                grid = same[:].rearrange("p (e g) -> p e g", e=E)
                pool.affine_select(out=grid, in_=grid, compare_op=ALU.is_ge, fill=0.0, base=0,
                                   pattern=[[-G, E], [0, G]], channel_multiplier=1).then_inc(made, 1)
                pool.wait_ge(made, 3)
                pool.affine_select(out=grid, in_=grid, compare_op=ALU.is_ge, fill=0.0, base=G - 1,
                                   pattern=[[G, E], [0, G]], channel_multiplier=-1).then_inc(made, 1)
                pool.wait_ge(made, 4)
                pool.affine_select(out=before[:], in_=same[:], compare_op=ALU.is_ge, fill=0.0, base=-1,
                                   pattern=[[1, P]], channel_multiplier=-1).then_inc(mats, 1)

            @block.tensor
            def _(te):
                te.wait_ge(mats, 2)
                te.wait_ge(packed_ok, 1)
                for s in range(SL):
                    te.transpose(big[s // 4][:, (s % 4) * P:(s % 4 + 1) * P], packed[:, s, :], ident[:]
                                 ).then_inc(turned, 1)
                with te.Fori(0, BITS) as i:
                    te.wait_ge(counted, i + 1)
                    te.matmul(tot[:, 0:1], same[:], cnt[:], start=True, stop=True).then_inc(summed, 1)
                te.wait_ge(chain, 3)
                te.matmul(tot[:, 1:2], same[:], cnt[:], start=True, stop=True)
                te.matmul(tot[:, 2:3], before[:], run[:, J - 1:J], start=True, stop=True).then_inc(sums, 1)
                te.wait_ge(chain, 8)
                te.matmul(tot[:, 3:4], before[:], pos[:, J - 1:J], start=True, stop=True).then_inc(sums, 1)
                te.wait_ge(chain, 10)
                for s in range(SL):
                    te.transpose(big[s // 4][:, (s % 4) * P:(s % 4 + 1) * P], run[:, s * P:(s + 1) * P], ident[:]
                                 ).then_inc(back, 1)

            @block.vector
            def _(dve):
                dve.wait_ge(const_ok, 2)
                dve.tensor_copy(packed[:].rearrange("p s (e g) -> p s e g", e=E), view).then_inc(packed_ok, 1)
                dve.wait_ge(turned, SL)
                for s in range(0, SL, 4):
                    dve.tensor_copy(sc[:, s * P:(s + 4) * P], big[s // 4][:]).then_inc(sc_ok, 1)
                dve.wait_ge(sc_ok, (SL + 3) // 4)
                with dve.Fori(0, BITS) as i:
                    dve.wait_ge(step, 3 * i + 1)
                    dve.tensor_tensor(cand[:], thr[:], bit[:], ALU.bitwise_or).then_inc(step, 1)
                    dve.wait_ge(step, 3 * i + 2)
                    dve.tensor_scalar(run[:], sc[:], cand[:].bitcast(F32), 0.0, ALU.is_ge, ALU.add,
                                      accum_out=cnt[:]).then_inc(counted, 1)
                    dve.tensor_scalar(bit[:], bit[:], 1, None, ALU.logical_shift_right).then_inc(step, 1)
                    dve.wait_ge(summed, i + 1)
                    dve.tensor_scalar(take[:], tot[:, 0:1], float(K), None, ALU.is_ge).then_inc(counted_take, 1)
                    dve.wait_ge(counted_take, i + 1)
                    dve.sem_inc(passed, 1)
                    dve.copy_predicated(thr[:], take[:], cand[:]).then_inc(step, 1)
                dve.wait_ge(step, 3 * BITS + 1)
                t = thr[:].bitcast(F32)
                dve.tensor_scalar(gt[:], sc[:], t, 0.0, ALU.is_gt, ALU.add, accum_out=cnt[:]).then_inc(chain, 1)
                dve.tensor_scalar(eq[:], sc[:], t, None, ALU.is_equal).then_inc(chain, 1)
                dve.wait_ge(chain, 2)
                dve.tensor_tensor_scan(run[:], ones[:], eq[:], 0.0, ALU.mult, ALU.add).then_inc(chain, 1)
                dve.wait_ge(sums, 1)
                dve.tensor_scalar(lim[:], tot[:, 1:2], -1.0, float(K), ALU.mult, ALU.add).then_inc(chain, 1)
                dve.wait_ge(chain, 4)
                dve.tensor_tensor(lim[:], lim[:], tot[:, 2:3], ALU.subtract).then_inc(chain, 1)
                dve.wait_ge(chain, 5)
                dve.scalar_tensor_tensor(eq[:], run[:], lim[:], eq[:], ALU.is_le, ALU.mult).then_inc(chain, 1)
                dve.wait_ge(chain, 6)
                dve.tensor_tensor(gt[:], gt[:], eq[:], ALU.add).then_inc(chain, 1)
                dve.wait_ge(chain, 7)
                dve.tensor_tensor_scan(pos[:], ones[:], gt[:], 0.0, ALU.mult, ALU.add).then_inc(chain, 1)
                dve.wait_ge(sums, 2)
                dve.tensor_copy(off[:], tot[:, 3:4]).then_inc(chain, 1)
                dve.wait_ge(chain, 9)
                dve.scalar_tensor_tensor(run[:], pos[:], off[:], gt[:], ALU.add, ALU.mult).then_inc(chain, 1)
                dve.wait_ge(back, SL)
                for s in range(0, SL, 4):
                    last = dve.tensor_scalar(slot[:, s * P:(s + 4) * P], big[s // 4][:], -1.0, None, ALU.add)
                last.then_inc(chain, 1)
                dve.wait_ge(chain, 11)
                dve.tensor_scalar(part[:], slot[:], P - 1, None, ALU.bitwise_and).then_inc(chain, 1)
                dve.tensor_scalar(slot[:], slot[:], 7, None, ALU.arith_shift_right).then_inc(chain, 1)
                dve.wait_ge(chain, 13)
                flat = "p s e g -> p (s e g)"
                dve.tensor_copy(d["lo"].rearrange(flat), part[:]).then_inc(chain, 1)
                dve.tensor_copy(d["hi"].rearrange(flat), slot[:]).then_inc(chain, 1)
                dve.wait_ge(chain, 15)


def stage3(nc, d, n_tok):
    E, G = 8, 16
    SL = n_tok // (G * P)
    K = n_tok // E
    NT = K // P
    NG = NT // 4
    FM = 8
    HR = 4
    FR = mybir.dt.float32r
    assert NG == 4 and SL == 8
    with ExitStack() as ctx:
        a = Alloc(nc, ctx)
        ident = a.sb("ident3", [P, P])
        counti = a.sb("counti", [P, P], I32)
        count = a.sb("count", [P, P], BF16)
        blki = a.sb("blki", [P, SL, G], I32)
        blk = a.sb("blk", [P, SL, G], BF16)
        pidi = a.sb("pidi", [P, 1], I32)
        pid = a.sb("pid", [P, 1])
        half = a.sb("half3", [P, 4])
        wraw = a.sb("wraw", [P, 2048])
        w1h = [a.sb(f"w1_upper{i}", [P, 2, 1024], FR) for i in range(2)]
        w1l = [a.sb(f"w1_rest{i}", [P, 2, 1024], FR) for i in range(2)]
        w2h = [a.sb(f"w2_upper{i}", [P, FM, 256], FR) for i in range(2)]
        w2l = [a.sb(f"w2_rest{i}", [P, FM, 256], FR) for i in range(2)]
        b1 = [a.sb(f"b1_{i}", [P, FM]) for i in range(2)]
        b2 = a.sb("b2", [P, E, 256])
        ln = a.sb("ln", [P, 2, 2])
        isin = a.sb("isin", [P, SL, G, 16], BF16)
        rhs = a.sb("rhs", [P, SL, G, 2, 16], BF16)
        onehot = [a.sb(f"onehot{i}", [P, G, P], BF16) for i in range(2)]
        idxf = a.sb("idxf", [P, 16])
        idx = [a.sb(f"idx{i}", [P, NT], I32) for i in range(2)]
        xg = [a.sb(f"xg{i}", [P, 4, 264]) for i in range(4)]
        xn = a.sb("xn", [P, 4, 256])
        stats = a.sb("stats3", [P, 4, 6])
        mv = a.sb("mv3", [P, 4, 2])
        ve = a.sb("ve3", [P, 4])
        rstd = a.sb("rstd3", [P, 4])
        yt, yth, ytl = a.sb("yt", [P, 2, 512]), a.sb("yt_upper", [P, 2, 512], FR), a.sb("yt_rest", [P, 2, 512], FR)
        hraw = a.sb("hraw", [P, HR, 512])
        hbh, hbl = a.sb("hidden_upper", [P, FM, 512], FR), a.sb("hidden_rest", [P, FM, 512], FR)
        ot = [a.sb(f"ot{i}", [P, 4, 256]) for i in range(2)]
        tp = [a.ps(f"tp{i}", [P, 512]) for i in range(2)]
        f1 = [a.ps(f"f1_{i}", [P, 512]) for i in range(2)]
        f2 = [a.ps(f"f2_{i}", [P, 512]) for i in range(2)]
        lists = a.ps("lists", [P, 32])
        S = a.sem
        pool_passed, dve_passed = S("pool_passed3"), S("dve_passed3")
        made, ident_ok, iotas, consts = S("made3"), S("ident3_ready"), S("iotas"), S("constants3")
        small_in, w_in, b1_in = S("small_in"), S("weights_in"), [S(f"bias_in{i}") for i in range(2)]
        rhs_ok, oh_ok, oh_used, idx_ok = S("rhs_steps"), S("onehot_ready"), S("onehot_used"), S("idx_ready")
        gathered = [S(f"rows_gathered{t}") for t in range(NG)]
        added = [S(f"rows_added{t}") for t in range(NG)]
        st, var_ok, rstd_ok, xn_ok = S("stats3_steps"), S("variance3"), S("rstd3_ready"), S("xn_ready")
        tp_ok, yt_ok = S("turned3"), S("yt_ready")
        f1_ok, gelu_ok, f2_ok = S("fc1_done"), S("gelu_done"), S("fc2_done")
        idxf_ok = S("idxf_ready")
        biased, ot_ok = S("biased"), S("out_rows_ready")
        w_upper, w_rest = S("weights_upper"), S("weights_rest")
        yt_rest, h_rest = S("yt_rest_ready"), {"dve": S("hidden_rest_dve"), "pool": S("hidden_rest_pool")}
        tiles_of = {"dve": range(0, 3), "pool": range(3, FM)}

        def rest_done(m, grp):
            who = "dve" if m in tiles_of["dve"] else "pool"
            return h_rest[who], grp * len(tiles_of[who]) + tiles_of[who].index(m) + 1

        def rest_of_hidden(eng, who, m, grp):
            eng.wait_ge(gelu_ok, grp * FM + m + 1)
            eng.tensor_tensor(hbl[:, m, :], hraw[:, m % HR, :], hbh[:, m, :].bitcast(F32),
                              ALU.subtract).then_inc(h_rest[who], 1)

        def flat(t):
            return t[:].rearrange("p k f -> p (k f)")

        with nc.Block() as block:

            def run(eng, prologue, step):
                prologue()
                for p in range(2):
                    for t in range(NG):
                        step(p, t, p, True, 2)
                with eng.Fori(1, E // 2 - 1) as j:
                    for p in range(2):
                        for t in range(NG):
                            step(2 * j + p, t, p, True, 2)
                for p in range(2):
                    for t in range(NG):
                        step(E - 2 + p, t, p, p == 0, min(2, NG - 1 - t) if p else 2)

            @block.sync
            def _(sp):
                sp.dma_start(ln[:], d["ln"]).then_inc(small_in, 16)
                sp.dma_start(b2[:].rearrange("p e f -> p (e f)"), d["b2"].partition_broadcast(P)).then_inc(small_in, 16)

                def load_weights(e, which):
                    if not (isinstance(e, int) and e == 0 and which == 0):
                        sp.wait_ge(w_rest, 2 * e + which)
                    src = d[("w1", "w2")[which]][bass.ds(e, 1)].rearrange("a p k f -> p (a k f)")
                    sp.dma_start(wraw[:], src).then_inc(w_in, 16)

                def load_bias(e, p):
                    sp.dma_start(b1[p][:], d["b1"][bass.ds(e, 1)].rearrange("a p k -> p (a k)")).then_inc(b1_in[p], 16)

                def prologue():
                    load_weights(0, 0)
                    load_bias(0, 0)
                    load_weights(0, 1)

                def step(e, t, p, following, ahead):
                    if not following:
                        return
                    if t == 0:
                        load_weights(e + 1, 0)
                        sp.wait_ge(f2_ok, e * NT + 4)
                        load_bias(e + 1, 1 - p)
                    if t == 1:
                        load_weights(e + 1, 1)

                run(sp, prologue, step)

            @block.gpsimd
            def _(pool):
                pool.memset(ident[:], 0.0).then_inc(made, 1)
                pool.memset(half[:], -0.5).then_inc(made, 1)
                pool.wait_ge(made, 2)
                pool.affine_select(out=ident[:], in_=ident[:], compare_op=ALU.not_equal, fill=1.0, base=0,
                                   pattern=[[-1, P]], channel_multiplier=1).then_inc(ident_ok, 1)
                pool.iota(counti[:], [[1, P]], base=0, channel_multiplier=0).then_inc(iotas, 1)
                pool.iota(blki[:], [[1, SL], [SL, G]], base=0, channel_multiplier=0).then_inc(iotas, 1)
                pool.iota(pidi[:], [[0, 1]], base=0, channel_multiplier=1).then_inc(iotas, 1)

                def gather(e, t, p):
                    grp = e * NG + t
                    if t == 0:
                        pool.wait_ge(idx_ok, e + 1)
                    if not isinstance(e, int) or e > 0:
                        pool.wait_ge(ot_ok, grp - 3)
                    pool.sem_inc(pool_passed, 1)
                    for b in range(4):
                        pool.indirect_dma_start(
                            out=xg[t][:, b, :], out_offset=None, in_=d["x1s"],
                            in_offset=bass.IndirectOffsetOnAxis(ap=idx[p][:, 4 * t + b:4 * t + b + 1], axis=0),
                        ).then_inc(gathered[t], 16)

                def power(grp):
                    pool.wait_ge(var_ok, grp + 1)
                    pool.tensor_tensor(rstd[:], ve[:], half[:], ALU.pow).then_inc(rstd_ok, 1)

                def prologue():
                    gather(0, 0, 0)
                    gather(0, 1, 0)
                    power(0)

                def step(e, t, p, following, ahead):
                    grp = e * NG + t
                    if ahead >= 1:
                        power(grp + 1)
                    for m in tiles_of["pool"]:
                        rest_of_hidden(pool, "pool", m, grp)
                    if ahead >= 2:
                        if t + 2 < NG:
                            gather(e, t + 2, p)
                        else:
                            gather(e + 1, t + 2 - NG, 1 - p)
                    pool.wait_ge(ot_ok, grp + 1)
                    if t == 0:
                        for k in range(NG):
                            pool.wait_ge(added[k], 64 * e)
                    pool.sem_inc(pool_passed, 1)
                    for b in range(4):
                        pool.indirect_dma_start(
                            out=d["acc"], out_offset=bass.IndirectOffsetOnAxis(
                                ap=idx[p][:, 4 * t + b:4 * t + b + 1], axis=0),
                            in_=ot[t % 2][:, b, :], in_offset=None, compute_op=ALU.add).then_inc(added[t], 16)

                run(pool, prologue, step)
                for k in range(NG):
                    pool.wait_ge(added[k], 64 * E)

            @block.scalar
            def _(act):
                act.wait_ge(small_in, 32)

                def turn_out(grp):
                    for k in range(2):
                        act.wait_ge(tp_ok, 2 * grp + k + 1)
                        if not isinstance(grp, int) or grp > 0:
                            act.wait_ge(yt_rest, 2 * (grp - 1) + k + 1)
                        for out in (yt, yth):
                            last = act.activation(out[:, k, :], tp[k][:], ACT.Identity, bias=ln[:, 1, k:k + 1],
                                                  scale=ln[:, 0, k:k + 1])
                        last.then_inc(yt_ok, 1)

                def step(e, t, p, following, ahead):
                    grp = e * NG + t
                    if t == 0:
                        act.wait_ge(b1_in[p], 8 * (e - p) + 16)
                    for m in range(FM):
                        act.wait_ge(f1_ok, grp * FM + m + 1)
                        if m == 0 and not (isinstance(e, int) and grp == 0):
                            act.wait_ge(f2_ok, grp * 4)
                        if m >= HR or not (isinstance(e, int) and grp == 0):
                            s, v = rest_done((m - HR) % FM, grp if m >= HR else grp - 1)
                            act.wait_ge(s, v)
                        for out in (hraw[:, m % HR, :], hbh[:, m, :]):
                            last = act.activation(out, f1[m % 2][:], ACT.Gelu_apprx_tanh, bias=b1[p][:, m:m + 1])
                        last.then_inc(gelu_ok, 1)
                    if ahead >= 1:
                        turn_out(grp + 1)

                run(act, lambda: turn_out(0), step)

            @block.tensor
            def _(te):
                te.wait_ge(ident_ok, 1)

                def token_list(e, slabs):
                    for s in slabs:
                        te.wait_ge(oh_ok, e * SL + s + 1)
                        if s == 0:
                            te.wait_ge(rhs_ok, 3 * e + 3)
                        for g in range(G):
                            last = te.matmul(lists[:], onehot[s % 2][:, g, :],
                                             rhs[:, s, g].rearrange("p a t -> p (a t)"),
                                             start=s == 0 and g == 0, stop=s == SL - 1 and g == G - 1)
                        last.then_inc(oh_used, 1)

                def turn(grp):
                    te.wait_ge(xn_ok, grp + 1)
                    for k in range(2):
                        if not isinstance(grp, int) or grp > 0:
                            te.wait_ge(yt_ok, 2 * (grp - 1) + k + 1)
                        for b in range(4):
                            last = te.transpose(tp[k][:, b * P:(b + 1) * P], xn[:, b, k * P:(k + 1) * P], ident[:])
                        last.then_inc(tp_ok, 1)

                def prologue():
                    token_list(0, range(SL))
                    turn(0)

                def step(e, t, p, following, ahead):
                    grp = e * NG + t
                    if t == 0:
                        te.wait_ge(w_rest, 2 * e + 2)
                    te.wait_ge(yt_rest, 2 * grp + 2)
                    for m in range(FM):
                        if m >= 2 or not (isinstance(e, int) and grp == 0):
                            te.wait_ge(gelu_ok, grp * FM + m - 1)
                        parts = [(w, y, k) for k in range(2) for w, y in (
                            (w1h[p], yth), (w1h[p], ytl), (w1l[p], yth))]
                        for i, (w, y, k) in enumerate(parts):
                            last = te.matmul(f1[m % 2][:], w[:, k, m * P:(m + 1) * P], y[:, k, :],
                                             start=i == 0, stop=i == len(parts) - 1)
                        last.then_inc(f1_ok, 1)
                    if following and t in (1, 2):
                        token_list(e + 1, range(4 * t - 2, 4 * t))
                    if ahead >= 1:
                        turn(grp + 1)
                    for b in range(4):
                        if not (isinstance(e, int) and grp == 0) and b % 2 == 0:
                            te.wait_ge(biased, 2 * (grp - 1) + b // 2 + 1)
                        rows = slice(b * P, (b + 1) * P)
                        out = f2[b // 2][:, (b % 2) * 256:(b % 2 + 1) * 256]
                        for m in range(FM):
                            if b == 0:
                                te.wait_ge(gelu_ok, grp * FM + m + 1)
                            te.matmul(out, hbh[:, m, rows], w2h[p][:, m, :], start=m == 0, stop=False)
                            te.matmul(out, hbh[:, m, rows], w2l[p][:, m, :], start=False, stop=False)
                        for m in range(FM):
                            if b == 0:
                                s, v = rest_done(m, grp)
                                te.wait_ge(s, v)
                            last = te.matmul(out, hbl[:, m, rows], w2h[p][:, m, :],
                                             start=False, stop=m == FM - 1)
                        last.then_inc(f2_ok, 1)
                        if following and t < 2 and b == 1:
                            token_list(e + 1, range(4 * t, 4 * t + 2))

                run(te, prologue, step)

            @block.vector
            def _(dve):
                dve.wait_ge(iotas, 3)
                dve.wait_ge(small_in, 32)
                for dst, src in ((count, counti), (blk, blki), (pid, pidi)):
                    dve.tensor_copy(dst[:], src[:]).then_inc(consts, 1)
                dve.wait_ge(consts, 3)

                def list_rhs(e):
                    hi = d["hi"][:, :, bass.ds(e, 1), :].rearrange("p s a g -> p s (a g)")
                    if not (isinstance(e, int) and e == 0):
                        dve.wait_ge(oh_used, e * SL)
                        dve.wait_ge(rhs_ok, 3 * e)
                    dve.tensor_tensor(isin[:], hi.unsqueeze(3).to_broadcast([P, SL, G, 16]),
                                      count[:, 0:16].unsqueeze(1).unsqueeze(1).to_broadcast([P, SL, G, 16]),
                                      ALU.is_equal).then_inc(rhs_ok, 1)
                    dve.wait_ge(rhs_ok, 3 * e + 1)
                    dve.tensor_tensor(rhs[:, :, :, 0, :], isin[:], blk[:].unsqueeze(3).to_broadcast([P, SL, G, 16]),
                                      ALU.mult).then_inc(rhs_ok, 1)
                    dve.tensor_scalar(rhs[:, :, :, 1, :], isin[:], pid[:, 0:1], None, ALU.mult).then_inc(rhs_ok, 1)

                def list_onehot(e, s):
                    if not (isinstance(e, int) and e == 0 and s < 2):
                        dve.wait_ge(oh_used, e * SL + s - 1)
                    lo = d["lo"][:, s, bass.ds(e, 1), :].rearrange("p a g -> p (a g)")
                    dve.tensor_tensor(onehot[s % 2][:], lo.unsqueeze(2).to_broadcast([P, G, P]),
                                      count[:].unsqueeze(1).to_broadcast([P, G, P]), ALU.is_equal).then_inc(oh_ok, 1)

                def list_index(e, p):
                    dve.wait_ge(oh_used, (e + 1) * SL)
                    dve.tensor_copy(idxf[:], lists[:, 16:32]).then_inc(idxf_ok, 1)
                    dve.wait_ge(idxf_ok, e + 1)
                    if not isinstance(e, int) or e > 1:
                        for k in range(NG):
                            dve.wait_ge(added[k], 64 * (e - 1))
                    dve.scalar_tensor_tensor(idx[p][:], lists[:, 0:16], float(P), idxf[:], ALU.mult, ALU.add
                                             ).then_inc(idx_ok, 1)

                def row_stats(grp, e, r):
                    dve.wait_ge(gathered[r], 64 * (e + 1))
                    if not isinstance(grp, int) or grp > 0:
                        dve.wait_ge(rstd_ok, grp)
                    for b in range(4):
                        last = dve.bn_stats(stats[:, b, :], xg[r][:, b, 0:256])
                    last.then_inc(st, 1)

                def variance(grp):
                    dve.wait_ge(st, 2 * grp + 1)
                    dve.sem_inc(dve_passed, 1)
                    for b in range(4):
                        last = dve.bn_aggr(mv[:, b, :], stats[:, b, :])
                    last.then_inc(st, 1)
                    dve.wait_ge(st, 2 * grp + 2)
                    dve.tensor_scalar(ve[:], mv[:, :, 1], LN_EPS, None, ALU.add).then_inc(var_ok, 1)

                def normalise(grp, r):
                    if not isinstance(grp, int) or grp > 0:
                        dve.wait_ge(tp_ok, 2 * grp)
                    dve.wait_ge(rstd_ok, grp + 1)
                    for b in range(4):
                        last = dve.tensor_scalar(xn[:, b, :], xg[r][:, b, 0:256], mv[:, b, 0:1], rstd[:, b:b + 1],
                                                 ALU.subtract, ALU.mult)
                    last.then_inc(xn_ok, 1)

                def split_weights(e, p, which):
                    upper = flat((w1h, w2h)[which][p])
                    dve.wait_ge(w_in, 16 * (2 * e + which) + 16)
                    dve.tensor_copy(upper, wraw[:]).then_inc(w_upper, 1)
                    dve.wait_ge(w_upper, 2 * e + which + 1)
                    dve.tensor_tensor(flat((w1l, w2l)[which][p]), wraw[:], upper.bitcast(F32), ALU.subtract
                                      ).then_inc(w_rest, 1)

                def rest_of_input(grp):
                    for k in range(2):
                        dve.wait_ge(yt_ok, 2 * grp + k + 1)
                        dve.tensor_tensor(ytl[:, k, :], yt[:, k, :], yth[:, k, :].bitcast(F32), ALU.subtract
                                          ).then_inc(yt_rest, 1)

                def prologue():
                    list_rhs(0)
                    for s in range(SL):
                        if s in (3, 6):
                            split_weights(0, 0, s // 3 - 1)
                        list_onehot(0, s)
                    list_index(0, 0)
                    row_stats(0, 0, 0)
                    variance(0)
                    normalise(0, 0)
                    rest_of_input(0)

                def step(e, t, p, following, ahead):
                    grp = e * NG + t
                    if ahead >= 1:
                        row_stats(grp + 1, e + (t + 1) // NG, (t + 1) % NG)
                        variance(grp + 1)
                    for m in tiles_of["dve"]:
                        rest_of_hidden(dve, "dve", m, grp)
                    if ahead >= 1:
                        normalise(grp + 1, (t + 1) % NG)
                    if following:
                        if t in (1, 2):
                            for s in range(4 * t - 2, 4 * t):
                                list_onehot(e + 1, s)
                            if t == 2:
                                list_index(e + 1, 1 - p)
                            split_weights(e + 1, 1 - p, t - 1)
                        if t == 0:
                            list_rhs(e + 1)
                        if t < 2:
                            for s in range(4 * t, 4 * t + 2):
                                list_onehot(e + 1, s)
                    if ahead >= 1:
                        rest_of_input(grp + 1)
                    if not isinstance(e, int) or grp > 1:
                        dve.wait_ge(added[(t - 2) % NG], 64 * (e + (1 if t >= 2 else 0)))
                    for i in range(2):
                        dve.wait_ge(f2_ok, grp * 4 + 2 * i + 2)
                        dve.tensor_tensor(ot[t % 2][:, 2 * i:2 * i + 2, :], f2[i][:].rearrange("p (b f) -> p b f", b=2),
                                          b2[:, bass.ds(e, 1), :].to_broadcast([P, 2, 256]), ALU.add).then_inc(biased, 1)
                    dve.wait_ge(biased, 2 * grp + 2)
                    for b in range(4):
                        s = xg[t][:, b, bass.ds(256 + e, 1)]
                        last = dve.tensor_scalar(ot[t % 2][:, b, :], ot[t % 2][:, b, :], s, None, ALU.mult)
                    last.then_inc(ot_ok, 1)

                run(dve, prologue, step)


def stage4(nc, d, n_tok):
    R, NBUF = 4, 8
    n = n_tok // (P * R)
    with ExitStack() as ctx:
        a = Alloc(nc, ctx)
        half = a.sb("half4", [P, R])
        x = [a.sb(f"rows{i}", [P, R, 256]) for i in range(NBUF)]
        stats = a.sb("stats4", [P, R, 6])
        mv = [a.sb(f"mv4_{i}", [P, R, 2]) for i in range(NBUF)]
        ve = [a.sb(f"ve4_{i}", [P, R]) for i in range(NBUF)]
        rstd = [a.sb(f"rstd4_{i}", [P, R]) for i in range(NBUF)]
        shift = [a.sb(f"shift4_{i}", [P, R]) for i in range(NBUF)]
        shift_ok = a.sem("shift4_ready")
        passed = a.sem("passed4")
        half_ok = a.sem("half4_ready")
        x_in = [a.sem(f"rows_in{i}") for i in range(NBUF)]
        x_out = [a.sem(f"rows_out{i}") for i in range(NBUF)]
        st, var_ok, rstd_ok, normed = a.sem("stats4_steps"), a.sem("variance4"), a.sem("rstd4_ready"), a.sem("normed4")
        view = d["acc"].rearrange("(n p r) f -> n p r f", p=P, r=R)
        out = d["out"].rearrange("(n p r) f -> n p r f", p=P, r=R)
        with nc.Block() as block:

            @block.sync
            def _(sp):
                def load(i, b):
                    sp.dma_start(x[b][:], view[bass.ds(i, 1)].rearrange("a p r f -> p (a r) f")).then_inc(x_in[b], 16)

                for b in range(NBUF):
                    load(b, b)
                with sp.Fori(1, n // NBUF) as j:
                    for b in range(NBUF):
                        sp.wait_ge(x_out[b], 16 * j)
                        load(NBUF * j + b, b)

            @block.scalar
            def _(act):
                with act.Fori(0, n // NBUF) as j:
                    for b in range(NBUF):
                        i = NBUF * j + b
                        act.wait_ge(shift_ok, i + 1)
                        for r in range(R):
                            last = act.activation(x[b][:, r, :], x[b][:, r, :], ACT.Identity,
                                                  bias=shift[b][:, r:r + 1], scale=rstd[b][:, r:r + 1])
                        last.then_inc(normed, 1)
                        act.wait_ge(normed, i + 1)
                        act.dma_start(out[bass.ds(i, 1)].rearrange("a p r f -> p (a r) f"), x[b][:]).then_inc(x_out[b], 16)
                for b in range(NBUF):
                    act.wait_ge(x_out[b], 16 * n // NBUF)

            @block.gpsimd
            def _(pool):
                pool.memset(half[:], -0.5).then_inc(half_ok, 1)
                pool.wait_ge(half_ok, 1)
                with pool.Fori(0, n // NBUF) as j:
                    for b in range(NBUF):
                        pool.wait_ge(var_ok, NBUF * j + b + 1)
                        pool.tensor_tensor(rstd[b][:], ve[b][:], half[:], ALU.pow).then_inc(rstd_ok, 1)

            @block.vector
            def _(dve):
                def row_stats(i, j, b):
                    dve.wait_ge(x_in[b], 16 * (j + 1))
                    for r in range(R):
                        last = dve.bn_stats(stats[:, r, :], x[b][:, r, :])
                    last.then_inc(st, 1)
                    dve.wait_ge(st, 2 * i + 1)
                    dve.sem_inc(passed, 1)
                    for r in range(R):
                        last = dve.bn_aggr(mv[b][:, r, :], stats[:, r, :])
                    last.then_inc(st, 1)
                    dve.wait_ge(st, 2 * i + 2)
                    dve.tensor_scalar(ve[b][:], mv[b][:, :, 1], LN_EPS, None, ALU.add).then_inc(var_ok, 1)

                def norm(i, b):
                    dve.wait_ge(rstd_ok, i + 1)
                    dve.scalar_tensor_tensor(shift[b][:], mv[b][:, :, 0], -1.0, rstd[b][:], ALU.mult, ALU.mult
                                             ).then_inc(shift_ok, 1)

                row_stats(0, 0, 0)
                with dve.Fori(0, n // NBUF - 1) as j:
                    for b in range(NBUF):
                        row_stats(NBUF * j + b + 1, j + (b + 1) // NBUF, (b + 1) % NBUF)
                        norm(NBUF * j + b, b)
                for b in range(NBUF):
                    if b + 1 < NBUF:
                        row_stats(n - NBUF + b + 1, n // NBUF - 1, b + 1)
                    norm(n - NBUF + b, b)


def program(nc, d, n_tok, n_batch):
    with ExitStack() as ctx:
        a = Alloc(nc, ctx)
        d["scores"] = a.sb("scores", [P, n_tok // P, 8])[:]
        stage1(nc, d, n_tok // CH, n_tok // n_batch // CH)
        d["lo"] = a.sb("lo", [P, n_tok // (16 * P), 8, 16], BF16)[:]
        d["hi"] = a.sb("hi", [P, n_tok // (16 * P), 8, 16], BF16)[:]
        stage2(nc, d, n_tok)
        stage3(nc, d, n_tok)
        stage4(nc, d, n_tok)


def kernel(**inputs):
    import numpy as np
    import concourse.bacc as bacc
    from concourse.bass_utils import run_bass_kernel_spmd

    c = np.ascontiguousarray
    at = {k[3:]: np.asarray(v) for k, v in inputs.items()}
    x = at["attn_hidden_states"]
    n_batch, seq, dm = x.shape
    n_tok = n_batch * seq
    xf = x.reshape(n_tok, dm)

    def tiles(w, n):
        return c(w.reshape((n, P) + w.shape[1:]).swapaxes(0, 1))

    vecs = np.stack([at["attn_conv1d_b"], at["attn_dt_proj_b"], at["attn_D_param"]])
    lnv = np.stack([at["ffn_ln_w"], at["ffn_ln_b"]])
    w1 = at["ffn_fc1s"].transpose(0, 2, 1)
    w2 = at["ffn_fc2s"].transpose(0, 2, 1)
    arrays = dict(
        x=c(xf), xt=c(xf.T), win=tiles(at["attn_in_proj_w"].T, 2), wconv=tiles(at["attn_conv1d_w"], 4),
        wx=tiles(at["attn_x_proj_w"].T, 4), wdt=c(at["attn_dt_proj_w"].T), wo=tiles(at["attn_out_proj_w"].T, 4),
        gate=tiles(at["ffn_gate_w"].T, 2), vecs=c(vecs.reshape(3, 4, P).transpose(2, 0, 1)),
        alog=tiles(at["attn_A_log"], 4),
        w1=c(w1.reshape(8, 2, P, 1024).transpose(0, 2, 1, 3)), w2=c(w2.reshape(8, 8, P, 256).transpose(0, 2, 1, 3)),
        b1=c(at["ffn_b1s"].reshape(8, 8, P).transpose(0, 2, 1)), b2=c(at["ffn_b2s"].reshape(8 * 256)),
        ln=c(lnv.reshape(2, 2, P).transpose(2, 0, 1)))
    nc = bacc.Bacc("TRN2", target_bir_lowering=False, num_devices=1)
    d = {k: nc.dram_tensor(f"in_{k}", v.shape, F32, kind="ExternalInput").ap() for k, v in arrays.items()}
    d["b_rows"] = nc.dram_tensor("b_rows", [2, 16, CH], F32).ap()
    d["x1s"] = nc.dram_tensor("x1_scores", [n_tok, 264], F32).ap()
    d["acc"] = nc.dram_tensor("sums", [n_tok, dm], F32).ap()
    d["out"] = nc.dram_tensor("out", [n_tok, dm], F32, kind="ExternalOutput").ap()
    program(nc, d, n_tok, n_batch)
    r = run_bass_kernel_spmd(nc, [{f"in_{k}": v for k, v in arrays.items()}], core_ids=[0])
    return r.results[0]["out"].reshape(n_batch, seq, dm)
```
